# Optimizing a Trainium2 kernel written in Bass

```python
import numpy as np
import jax
import jax.numpy as jnp

def _softmax(x, axis=-1):
    return jax.nn.softmax(x, axis=axis)

def _gelu(x):
    return jax.nn.gelu(x, approximate=True)

def _silu(x):
    return jax.nn.silu(x)

def _sigmoid(x):
    return jax.nn.sigmoid(x)

def _layernorm(x, axis=-1, eps=1e-05):
    m = jnp.mean(x, axis=axis, keepdims=True)
    v = jnp.var(x, axis=axis, keepdims=True)
    return (x - m) / jnp.sqrt(v + eps)

def _scatter_add(tgt, idx, src, axis=0):
    return tgt.at[idx].add(src)

def _segment_sum(src, seg, n):
    return jax.ops.segment_sum(src, seg, n)
kernel_name = 'mk_seq_postln_d1_jaxref_r2_416656'

def setup_inputs(seed: int=0):
    np.random.seed(seed)
    _w = jnp.asarray

    def _L0_attn_setup():
        import jax, jax.numpy as jnp
        import numpy as np
        B, S, E, H, G = (2, 1024, 1024, 16, 4)
        D = E // H
        key = jax.random.key(seed)
        ks = jax.random.split(key, 7)
        scale = 1.0 / np.sqrt(E)
        x = jax.random.normal(ks[0], (B, S, E), dtype=jnp.float32)
        Wq = jax.random.normal(ks[1], (H, E, D), dtype=jnp.float32) * scale
        bq = jax.random.normal(ks[2], (H, D), dtype=jnp.float32) * 0.02
        Wk = jax.random.normal(ks[3], (G, E, D), dtype=jnp.float32) * scale
        bk = jax.random.normal(ks[4], (G, D), dtype=jnp.float32) * 0.02
        Wv = jax.random.normal(ks[5], (G, E, D), dtype=jnp.float32) * scale
        bv = jax.random.normal(ks[6], (G, D), dtype=jnp.float32) * 0.02
        return {'x': x, 'Wq': Wq, 'bq': bq, 'Wk': Wk, 'bk': bk, 'Wv': Wv, 'bv': bv}
    _L0_attn_in = _L0_attn_setup()

    def _L0_ffn_setup():
        import jax, jax.numpy as jnp
        import numpy as np
        DIM = 1024
        N_EXPERTS = 8
        TOP_K = 2
        key = jax.random.key(seed)
        ks = jax.random.split(key, 5)
        x = jax.random.normal(ks[0], (4, 2048, DIM), dtype=jnp.float32)
        W_up = jax.random.normal(ks[1], (DIM, DIM), dtype=jnp.float32) * (1.0 / np.sqrt(DIM))
        W_down = jax.random.normal(ks[2], (DIM, DIM), dtype=jnp.float32) * (1.0 / np.sqrt(DIM))
        W_gate = jax.random.normal(ks[3], (N_EXPERTS, DIM), dtype=jnp.float32) * (1.0 / np.sqrt(DIM))
        W_expert = jax.random.normal(ks[4], (DIM, DIM), dtype=jnp.float32) * (1.0 / np.sqrt(DIM))
        return {'x': x, 'W_up': W_up, 'W_down': W_down, 'W_gate': W_gate, 'W_expert': W_expert}
    _L0_ffn_in = _L0_ffn_setup()
    _d = {'L0_attn_x': _L0_attn_in['x'], 'L0_attn_Wq': _L0_attn_in['Wq'], 'L0_attn_bq': _L0_attn_in['bq'], 'L0_attn_Wk': _L0_attn_in['Wk'], 'L0_attn_bk': _L0_attn_in['bk'], 'L0_attn_Wv': _L0_attn_in['Wv'], 'L0_attn_bv': _L0_attn_in['bv'], 'L0_ffn_W_up': _L0_ffn_in['W_up'], 'L0_ffn_W_down': _L0_ffn_in['W_down'], 'L0_ffn_W_gate': _L0_ffn_in['W_gate'], 'L0_ffn_W_expert': _L0_ffn_in['W_expert']}
    _x0 = _d['L0_attn_x']
    _d['L0_attn_x'] = jax.random.normal(jax.random.fold_in(jax.random.key(seed), 1), (4, 1024, 1024), dtype=_x0.dtype)
    del _x0
    return _d

def reference(L0_attn_x, L0_attn_Wq, L0_attn_bq, L0_attn_Wk, L0_attn_bk, L0_attn_Wv, L0_attn_bv, L0_ffn_W_up, L0_ffn_W_down, L0_ffn_W_gate, L0_ffn_W_expert):

    def _L0_attn_ref(x, Wq, bq, Wk, bk, Wv, bv):
        import jax, jax.numpy as jnp
        import numpy as np
        B, S, E, H, G = (2, 1024, 1024, 16, 4)
        D = E // H
        h, e, d = Wq.shape
        g = Wk.shape[0]
        per = h // g
        s = x.shape[1]
        q = jnp.einsum('bse,hed->bhsd', x, Wq) + bq[None, :, None, :]
        kg = jnp.einsum('bse,ged->bgsd', x, Wk) + bk[None, :, None, :]
        vg = jnp.einsum('bse,ged->bgsd', x, Wv) + bv[None, :, None, :]
        k = jnp.repeat(kg, per, axis=1)
        v = jnp.repeat(vg, per, axis=1)
        scores = jnp.einsum('bhqd,bhkd->bhqk', q, k) * (1.0 / np.sqrt(d))
        causal = jnp.triu(jnp.ones((s, s), dtype=bool), k=1)
        scores = jnp.where(causal[None, None, :, :], -jnp.inf, scores)
        attn = jax.nn.softmax(scores, axis=-1)
        out = jnp.einsum('bhqk,bhkd->bhqd', attn, v)
        return out.transpose(0, 2, 1, 3).reshape(x.shape[0], s, h * d)

    def _L0_ffn_ref(x, W_up, W_down, W_gate, W_expert):
        import jax, jax.numpy as jnp
        import numpy as np
        DIM = 1024
        N_EXPERTS = 8
        TOP_K = 2
        logits = jnp.einsum('bsd,ed->bse', x, W_gate)
        routing_weights, selected_experts = jax.lax.top_k(logits, TOP_K)
        shared_out = jnp.einsum('bsd,od->bso', jax.nn.relu(jnp.einsum('bsd,od->bso', x, W_up)), W_down)
        rw = jax.nn.softmax(routing_weights, axis=-1)
        expert_out = jnp.einsum('bsd,do->bso', x, W_expert)
        moe_out = jnp.sum(rw, axis=-1, keepdims=True) * expert_out
        return shared_out + moe_out
    x = L0_attn_x
    x = _layernorm(x + _L0_attn_ref(x, L0_attn_Wq, L0_attn_bq, L0_attn_Wk, L0_attn_bk, L0_attn_Wv, L0_attn_bv), axis=-1)
    x = _layernorm(x + _L0_ffn_ref(x, L0_ffn_W_up, L0_ffn_W_down, L0_ffn_W_gate, L0_ffn_W_expert), axis=-1)
    return x

_drawn_inputs = setup_inputs


def setup_inputs(seed=0):
    import zlib

    import numpy as np

    out = dict(_drawn_inputs(seed))
    spreads = {}
    factors = {'L0_attn_bq': 27.131, 'L0_attn_bk': 64.0, 'L0_attn_bv': 2.82, 'L0_ffn_W_gate': 64.0}
    for name, (base, spread) in spreads.items():
        noise = np.random.default_rng([zlib.crc32(name.encode()), seed]).standard_normal(out[name].shape)
        drawn = base * np.exp(spread * noise) if base else spread * noise
        out[name] = jnp.asarray(drawn.astype(out[name].dtype))
    for name, factor in factors.items():
        out[name] = (out[name] * factor).astype(out[name].dtype)
    return out
```

```python
from contextlib import ExitStack

import numpy as np

import concourse.bass as bass
from concourse import mybir
from concourse.alu_op_type import AluOpType as ALU

F32 = mybir.dt.float32
F32R = mybir.dt.float32r
BF16 = mybir.dt.bfloat16
ACT = mybir.ActivationFunctionType
AX = mybir.AxisListType
P = 128
EPS = 1e-5
MASKED = -3.0e38


class Names:
    pass


def raw(ap):
    return ap.bitcast(F32)


def constants(nc, c, bank):
    made = c.enter_context(nc.semaphore("constants_made"))
    with nc.Block() as block:

        @block.gpsimd
        def _(pool):
            pool.memset(bank.ident[:, :], 0.0).then_inc(made, 1)
            pool.memset(bank.ident_bf[:, :], 0.0).then_inc(made, 1)
            pool.memset(bank.mask[:, :], 0.0).then_inc(made, 1)
            pool.wait_ge(made, 3)
            for m in (bank.ident, bank.ident_bf):
                pool.affine_select(out=m[:, :], in_=m[:, :], compare_op=ALU.not_equal, fill=1.0, base=0,
                                   pattern=[[-1, P]], channel_multiplier=1).then_inc(made, 1)
            pool.affine_select(out=bank.mask[:, :], in_=bank.mask[:, :], compare_op=ALU.is_ge, fill=MASKED, base=0,
                               pattern=[[-1, P]], channel_multiplier=1).then_inc(made, 1)
            pool.wait_ge(made, 6)


def stage_a(nc, dims, dram, const, psum):
    D, H, G, HD, S, B = dims.D, dims.H, dims.G, dims.HD, dims.S, dims.B
    KC = D // P
    CH = 512
    TPC = CH // P
    NQ, NK = H * HD // P, G * HD // P
    NQK = NQ + NK
    NG = NQK + TPC
    NT = 2 * TPC
    KV = G * HD
    RING, SLOTS = 4, 4
    SCALE = 1.0 / float(np.sqrt(HD))
    with ExitStack() as c:
        def sb(name, shape, dt=F32):
            return c.enter_context(nc.sbuf_tensor(name, shape, dt))

        def sem(name):
            return c.enter_context(nc.semaphore(name))

        wq = sb("wq", [P, 2, KC, D], F32R)
        wk = sb("wk", [P, 2, KC, KV], F32R)
        wv = sb("wv", [P, 2, KC, KV], F32R)
        xt = sb("xt", [P, 2, 2, KC, CH], F32R)
        x_raw = sb("x_raw", [P, 2, D])
        w_raw = sb("w_raw", [P, 2, D])
        stage = sb("stage", [P, SLOTS, 2, CH], F32R)
        v_sum = sb("v_sum", [P, 2, KV])
        v_out = sb("v_out", [P, 2, G, 2, HD], F32R)
        bias = sb("bias", [P, NQK])
        bias_s = sb("bias_s", [P, NQK])
        bias_v = sb("bias_v", [P, KV])
        x_in = [sem(f"a_x_in{i}") for i in range(2)]
        w_in = [sem(f"a_w_in{i}") for i in range(2)]
        bias_in = sem("a_bias_in")
        bias_scaled = sem("a_bias_scaled")
        w_hi, w_lo = sem("a_w_hi"), sem("a_w_lo")
        t_done, t_hi, t_lo = sem("a_t_done"), sem("a_t_hi"), sem("a_t_lo")
        group_done = sem("a_group_done")
        qk_hi = sem("a_qk_hi")
        drained = sem("a_drained")
        stored = [sem(f"a_stored{i}") for i in range(SLOTS)]
        v_hi = sem("a_v_hi")
        v_lo = sem("a_v_lo")
        v_stored = [sem(f"a_v_stored{i}") for i in range(2)]

        NCH = B * S // CH
        x_tiles = dram.x
        w_pieces = KC + KC // 2

        def piece(i):
            src = w_raw[:, i % 2, :]
            if i < KC:
                return [(wq[:, 0, i, :], wq[:, 1, i, :], src, SCALE)]
            j = i - KC
            v = src.rearrange("p (a s n) -> p a s n", a=2, s=2)
            return [(w[:, 0, 2 * j:2 * j + 2, :], w[:, 1, 2 * j:2 * j + 2, :], v[:, a], 1.0)
                    for a, w in enumerate((wk, wv))]

        with nc.Block() as block:

            @block.sync
            def _(sp):
                def load_x(tile, slot):
                    sp.dma_start(x_raw[:, slot, :],
                                 x_tiles[bass.ds(tile, 1), :, :].rearrange("a p n -> (a p) n")
                                 ).then_inc(x_in[slot], 16)

                load_x(0, 0)
                load_x(1, 1)
                for i in range(2, 6):
                    sp.wait_ge(t_done, 2 * (i - 1))
                    load_x(i, i % 2)

                def chunk(k, par, t_next, x_next):
                    ch = 2 * k + par
                    for n in range(NQK):
                        m = NQK * par + n
                        slot = m % SLOTS
                        sp.wait_ge(drained, 2 * NG * k + NG * par + n + 1 + RING)
                        for z in range(2):
                            if n < NQ:
                                g, hh = n // 2, 2 * (n % 2)
                                dst = dram.q[bass.ds(k * G + g, 1), hh:hh + 2, z * HD:(z + 1) * HD,
                                             par * CH:(par + 1) * CH].rearrange("a h d t -> (a h) d t")
                            else:
                                dst = dram.k[bass.ds(k * G + 2 * (n - NQ), 2), z, :, par * CH:(par + 1) * CH]
                            sp.dma_start(dst, raw(stage[:, slot, z, :])).then_inc(stored[slot], 16)
                        i = n // 2 + 2
                        if n % 2 == 1 and n < NT and (t_next if i < TPC else x_next):
                            sp.wait_ge(t_done, NT * ch + NT + n + 1)
                            load_x(TPC * ch + TPC + i, i % 2)
                    for i in range(TPC):
                        m = TPC * par + i
                        sp.wait_ge(v_lo, 2 * TPC * k + m + 1 + 2)
                        dst = dram.v[bass.ds(k * G, G), (TPC * par + i) * P:(TPC * par + i + 1) * P, :]
                        sp.dma_start(dst.rearrange("g t f -> t g f"),
                                     raw(v_out[:, i % 2]).rearrange("p g z d -> p g (z d)")
                                     ).then_inc(v_stored[i % 2], 16)

                with sp.Fori(0, NCH // 2 - 1) as k:
                    chunk(k, 0, True, True)
                    chunk(k, 1, True, True)
                k = NCH // 2 - 1
                chunk(k, 0, True, False)
                chunk(k, 1, False, False)
                for s in range(SLOTS):
                    sp.wait_ge(stored[s], 32 * NQK * NCH // SLOTS + 1)
                for s in range(2):
                    sp.wait_ge(v_stored[s], 16 * TPC * NCH // 2 + 1)

            @block.scalar
            def _(act):
                for m in range(NQ):
                    act.dma_start(bias[:, m:m + 1], dram.bq[m * P:(m + 1) * P, :]).then_inc(bias_in, 16)
                for m in range(NK):
                    act.dma_start(bias[:, NQ + m:NQ + m + 1], dram.bk[m * P:(m + 1) * P, :]).then_inc(bias_in, 16)
                act.dma_start(bias_v[:, :], dram.bv.broadcast_to([P, KV])).then_inc(bias_in, 16)

                def load_w(i):
                    dst = w_raw[:, i % 2, :]
                    if i < KC:
                        act.dma_start(dst.rearrange("p (h d) -> p h d", d=HD),
                                      dram.wq[:, i * P:(i + 1) * P, :].rearrange("h p d -> p h d")
                                      ).then_inc(w_in[i % 2], 16)
                        return
                    j = i - KC
                    for a, w in enumerate((dram.wk, dram.wv)):
                        for s in range(2):
                            e = (2 * j + s) * P
                            act.dma_start(dst[:, (2 * a + s) * KV:(2 * a + s + 1) * KV].rearrange("p (g d) -> p g d", d=HD),
                                          w[:, e:e + P, :].rearrange("g p d -> p g d")).then_inc(w_in[i % 2], 16)

                load_w(0)
                load_w(1)

                def t_high(n, par, count):
                    act.wait_ge(t_done, count + 1)
                    act.activation(xt[:, par, 0, 4 * (n % 2):4 * (n % 2) + 4, (n // 2) * P:(n // 2 + 1) * P],
                                   psum[:, n % 2, :].rearrange("p (a t) -> p a t", a=4), ACT.Copy).then_inc(t_hi, 1)

                for n in range(NT):
                    t_high(n, 0, n)
                arrived = [0, 0]
                for i in range(w_pieces):
                    arrived[i % 2] += 16 if i < KC else 64
                    act.wait_ge(w_in[i % 2], arrived[i % 2])
                    for hi, lo, src, scale in piece(i):
                        done = act.activation(hi, src, ACT.Copy, scale=scale)
                    done.then_inc(w_hi, 1)
                    if i + 2 < w_pieces:
                        act.wait_ge(w_lo, i + 1)
                        act.wait_ge(w_hi, i + 1)
                        load_w(i + 2)
                act.wait_ge(bias_scaled, 1)

                def chunk(k, par, t_next):
                    ch = 2 * k + par
                    for n in range(NG):
                        bank = 2 + (NG * par + n) % RING
                        if n < NQK:
                            m = NQK * par + n
                            act.wait_ge(group_done, 2 * NG * k + NG * par + n + 1)
                            act.wait_ge(stored[m % SLOTS], 2 * NQK // SLOTS * 32 * k + 32 * (m // SLOTS) + 1)
                            act.activation(stage[:, m % SLOTS, 0, :], psum[:, bank, :], ACT.Identity,
                                           bias=bias_s[:, n:n + 1]).then_inc(qk_hi, 1)
                        else:
                            i = n - NQK
                            m = TPC * par + i
                            act.wait_ge(drained, 2 * NG * k + NG * par + n + 1 + RING)
                            act.wait_ge(v_stored[i % 2], 16 * (TPC * k + m // 2) + 1)
                            act.activation(v_out[:, i % 2, :, 0, :],
                                           v_sum[:, i % 2, :].rearrange("p (g d) -> p g d", d=HD),
                                           ACT.Copy).then_inc(v_hi, 1)
                        if n < NT and t_next:
                            t_high(n, 1 - par, NT * ch + NT + n)

                with act.Fori(0, NCH // 2 - 1) as k:
                    chunk(k, 0, True)
                    chunk(k, 1, True)
                chunk(NCH // 2 - 1, 0, True)
                chunk(NCH // 2 - 1, 1, False)

            @block.vector
            def _(dve):
                dve.sem_inc(drained, RING)
                for s in range(SLOTS):
                    dve.sem_inc(stored[s], 1)
                for s in range(2):
                    dve.sem_inc(v_stored[s], 1)
                dve.sem_inc(v_lo, 2)

                def t_low(n, par, count):
                    dve.wait_ge(t_hi, count + 1)
                    cols = (slice(4 * (n % 2), 4 * (n % 2) + 4), slice((n // 2) * P, (n // 2 + 1) * P))
                    dve.tensor_tensor(xt[:, par, 1, cols[0], cols[1]],
                                      psum[:, n % 2, :].rearrange("p (a t) -> p a t", a=4),
                                      raw(xt[:, par, 0, cols[0], cols[1]]), ALU.subtract).then_inc(t_lo, 1)

                for n in range(NT):
                    t_low(n, 0, n)
                for i in range(w_pieces):
                    dve.wait_ge(w_hi, i + 1)
                    for hi, lo, src, scale in piece(i):
                        done = dve.scalar_tensor_tensor(lo, src, scale, raw(hi), op0=ALU.mult, op1=ALU.subtract)
                    done.then_inc(w_lo, 1)
                dve.wait_ge(bias_in, 16 * (NQK + 1))
                dve.tensor_scalar(bias_s[:, 0:NQ], bias[:, 0:NQ], SCALE, None, ALU.mult)
                dve.tensor_copy(bias_s[:, NQ:NQK], bias[:, NQ:NQK]).then_inc(bias_scaled, 1)
                dve.wait_ge(bias_scaled, 1)

                def chunk(k, par, t_next):
                    ch = 2 * k + par
                    for n in range(NG):
                        bank = 2 + (NG * par + n) % RING
                        if n < NQK:
                            m = NQK * par + n
                            dve.wait_ge(qk_hi, 2 * NQK * k + m + 1)
                            dve.scalar_tensor_tensor(stage[:, m % SLOTS, 1, :], psum[:, bank, :], bias_s[:, n:n + 1],
                                                     raw(stage[:, m % SLOTS, 0, :]), op0=ALU.add,
                                                     op1=ALU.subtract).then_inc(drained, 1)
                        else:
                            i = n - NQK
                            m = TPC * par + i
                            dve.wait_ge(group_done, 2 * NG * k + NG * par + n + 1)
                            dve.wait_ge(v_lo, 2 * TPC * k + m + 1)
                            dve.tensor_tensor(v_sum[:, i % 2, :], psum[:, bank, 0:KV], bias_v[:, :],
                                              ALU.add).then_inc(drained, 1)
                        if n < NT and t_next:
                            t_low(n, 1 - par, NT * ch + NT + n)

                with dve.Fori(0, NCH // 2 - 1) as k:
                    chunk(k, 0, True)
                    chunk(k, 1, True)
                chunk(NCH // 2 - 1, 0, True)
                chunk(NCH // 2 - 1, 1, False)

            @block.gpsimd
            def _(pool):
                with pool.Fori(0, NCH) as ch:
                    for i in range(TPC):
                        pool.wait_ge(v_hi, TPC * ch + i + 1)
                        pool.tensor_tensor(v_out[:, i % 2, :, 1, :],
                                           v_sum[:, i % 2, :].rearrange("p (g d) -> p g d", d=HD),
                                           raw(v_out[:, i % 2, :, 0, :]), ALU.subtract).then_inc(v_lo, 1)

            @block.tensor
            def _(pe):
                def turn(n, ch):
                    i = n // 2
                    if n % 2 == 0:
                        pe.wait_ge(x_in[i % 2], 16 * (TPC // 2 * ch + i // 2 + 1))
                    if not (isinstance(ch, int) and NT * ch + n < 2):
                        pe.wait_ge(t_lo, NT * ch + n - 1)
                    for a in range(4):
                        e = 4 * (n % 2) + a
                        done = pe.transpose(psum[:, n % 2, a * P:(a + 1) * P], x_raw[:, i % 2, e * P:(e + 1) * P],
                                            const.ident[:, :])
                    done.then_inc(t_done, 1)

                for n in range(NT):
                    turn(n, 0)
                pe.wait_ge(w_lo, w_pieces)
                pe.wait_ge(w_hi, w_pieces)

                def chunk(k, par, t_next):
                    ch = 2 * k + par
                    pe.wait_ge(t_lo, NT * ch + NT)
                    for n in range(NG):
                        bank = 2 + (NG * par + n) % RING
                        pe.wait_ge(drained, 2 * NG * k + NG * par + n + 1)
                        for e in range(KC):
                            for zw, zx in ((0, 0), (0, 1), (1, 0)):
                                first, last = e == 0 and zw + zx == 0, e == KC - 1 and zw == 1
                                if n < NQ:
                                    out, lhs, rhs = psum[:, bank, :], wq[:, zw, e, n * P:(n + 1) * P], xt[:, par, zx, e, :]
                                elif n < NQK:
                                    o = (n - NQ) * P
                                    out, lhs, rhs = psum[:, bank, :], wk[:, zw, e, o:o + P], xt[:, par, zx, e, :]
                                else:
                                    o = (n - NQK) * P
                                    out, lhs, rhs = psum[:, bank, 0:KV], xt[:, par, zx, e, o:o + P], wv[:, zw, e, :]
                                done = pe.matmul(out, lhs, rhs, start=first, stop=last)
                        done.then_inc(group_done, 1)
                        if n < NT and t_next:
                            turn(n, ch + 1)

                with pe.Fori(0, NCH // 2 - 1) as k:
                    chunk(k, 0, True)
                    chunk(k, 1, True)
                chunk(NCH // 2 - 1, 0, True)
                chunk(NCH // 2 - 1, 1, False)


def stage_b(nc, dims, dram, const, psum):
    G, HD, S, B = dims.G, dims.HD, dims.S, dims.B
    R = dims.H // G
    NT = S // P
    STEPS = 2 * NT
    LEAD = 2
    SLOTS = 4
    TR = 3
    S_BANKS, T_BANK, O_BANK = 0, 4, 7
    LOOPS = B * G // 2
    assert R * P == 512 and STEPS % SLOTS == 0

    def tile_of(step):
        s = step % STEPS
        return s if s < NT else STEPS - 1 - s

    def key_blocks(step):
        return tile_of(step) + 1

    BLOCKS = sum(key_blocks(s) for s in range(STEPS))
    TURNS = BLOCKS + STEPS
    assert BLOCKS % TR == 0

    def order(step, scores):
        n, todo = key_blocks(step), []
        for j in range(n):
            todo += [("scores", h) for h in range(R) if h * n // R == j and scores]
            todo.append(("turn", j))
            if j >= 2:
                todo.append(("pv", j - 2))
        todo += [("pv", j) for j in range(max(n - 2, 0), n)]
        return todo + [("out", 0)]

    def before(step, out):
        return sum(key_blocks(s) + out for s in range(step))

    def use_before(use):
        return use - TR if use >= TR else \
            max(u for u in range(TURNS) if u % TR == use % TR) - TURNS

    with ExitStack() as c:
        def sb(name, shape, dt=F32):
            return c.enter_context(nc.sbuf_tensor(name, shape, dt))

        def sem(name):
            return c.enter_context(nc.semaphore(name))

        q = sb("q_sb", [P, 2, R, S], F32R)
        kk = sb("k_sb", [P, 2, 2, S], F32R)
        v = sb("v_sb", [P, 2, NT, 2 * HD], F32R)
        probs = sb("probs", [P, SLOTS, R, S])
        pt = sb("pt", [P, TR, 2, R * P], F32R)
        top = sb("top", [P, SLOTS * R])
        sums = sb("sums", [P, SLOTS * R])
        inv = sb("inv", [P, 2, R])
        o_t = sb("o_t", [P, 2, R * P])
        o_n = sb("o_n", [P, 2, R, 2 * HD])
        o_sum = sb("o_sum", [P, 2, R, HD])
        res = sb("res", [P, 2, R, HD])
        qk_in = [sem(f"b_qk_in{i}") for i in range(2)]
        v_in = [sem(f"b_v_in{i}") for i in range(2)]
        scored, topped, expd = sem("b_scored"), sem("b_topped"), sem("b_expd")
        turned, hi_done = sem("b_turned"), sem("b_hi_done")
        t_free = sem("b_t_free")
        pv_done, o_copied = sem("b_pv_done"), sem("b_o_copied")
        inverted, summed, scaled = sem("b_inverted"), sem("b_summed"), sem("b_scaled")
        stored = [sem(f"b_stored{i}") for i in range(2)]
        idle = sem("b_idle")

        with nc.Block() as block:

            @block.sync
            def _(sp):
                def load_qk(g, par):
                    def at(x):
                        return x[bass.ds(g, 1)]
                    sp.dma_start(raw(q[:, par]), at(dram.q).rearrange("a h p t -> (a p) h t")).then_inc(qk_in[par], 16)
                    for half in range(2):
                        sp.dma_start(raw(kk[half * HD:(half + 1) * HD, par]),
                                     at(dram.k).rearrange("a z p t -> (a p) z t")).then_inc(qk_in[par], 16)

                def load_v(g, par):
                    sp.dma_start(raw(v[:, par]), dram.v[bass.ds(g, 1)].rearrange("a (j p) f -> p (a j) f", p=P)
                                 ).then_inc(v_in[par], 16)

                for g in range(2):
                    load_qk(g, g)
                    load_v(g, g)

                def body(k, last):
                    for s in range(STEPS):
                        gp, tile = s // NT, tile_of(s)
                        sp.wait_ge(scaled, STEPS * k + s + 1 + 2)
                        sp.sem_inc(idle, 1)
                        sp.dma_start(dram.att[bass.ds(k // (G // 2), 1), tile * P:(tile + 1) * P,
                                              bass.ds(2 * (k % (G // 2)) + gp, 1), :].rearrange("a t g n -> t (a g n)"),
                                     res[:, s % 2].rearrange("p h d -> p (h d)")).then_inc(stored[s % 2], 16)
                        if last:
                            continue
                        if s in (NT - LEAD, STEPS - LEAD):
                            sp.wait_ge(scored, R * (STEPS * k + s + LEAD))
                            load_qk(2 * k + 2 + s // NT, s // NT)
                        if s in (NT, STEPS - 1):
                            at = NT if s == NT else STEPS
                            sp.wait_ge(pv_done, BLOCKS * k + before(at, 0))
                            load_v(2 * k + 2 + (s > NT), int(s > NT))

                with sp.Fori(0, LOOPS - 1) as k:
                    body(k, False)
                body(LOOPS - 1, True)
                for i in range(2):
                    sp.wait_ge(stored[i], 16 * STEPS * LOOPS // 2 + 1)

            def scores_at(step):
                return (step + LEAD) // STEPS, (step + LEAD) % STEPS

            def view(ap, n):
                w = n * P if n * P <= 512 else n * P // 2
                return ap[:, 0:n * P // w, 0:w], w

            @block.tensor
            def _(pe):
                def scores(k, s, h):
                    gp, n, slot = s // NT, key_blocks(s), h % 2
                    if h == 0 and s in (0, NT):
                        pe.wait_ge(qk_in[gp], 48 * (k + 1))
                    if not (isinstance(k, int) and R * (STEPS * k + s) + h < 2):
                        pe.wait_ge(expd, R * (STEPS * k + s) + h - 1)
                    w = view(psum[:, 0:2, :], n)[1]
                    for part in range(n * P // w):
                        bank = S_BANKS + 2 * slot + part
                        lhs = q[:, gp, h, tile_of(s) * P:(tile_of(s) + 1) * P]
                        keys = slice(part * w, (part + 1) * w)
                        pe.matmul(psum[:, bank, 0:w], lhs, kk[:, gp, 0, keys], start=True, stop=False)
                        if keys.stop == n * P:
                            pe.matmul(psum[:, bank, w - P:w], const.ident_bf[:, :], const.mask[:, :],
                                      start=False, stop=False)
                        done = pe.matmul(psum[:, bank, 0:w], lhs, kk[:, gp, 1, keys], start=False, stop=True)
                    done.then_inc(scored, 1)

                for s in range(LEAD):
                    for h in range(R):
                        scores(0, s, h)

                def body(k, last):
                    for s in range(STEPS):
                        gp, n = s // NT, key_blocks(s)
                        dk, s2 = scores_at(s)
                        for what, j in order(s, not (last and dk)):
                            use = before(s, 1) + (j if what == "turn" else n)
                            block_no = before(s, 0) + j
                            if what == "scores":
                                scores(k + dk, s2, j)
                            elif what == "turn":
                                if j == 0:
                                    pe.wait_ge(expd, R * (STEPS * k + s + 1))
                                pe.wait_ge(t_free, TURNS * k + use_before(use) + 1 + TR)
                                for h in range(R):
                                    done = pe.transpose(psum[:, T_BANK + use % TR, h * P:(h + 1) * P],
                                                        probs[:, s % SLOTS, h, j * P:(j + 1) * P], const.ident[:, :])
                                done.then_inc(turned, 1)
                            elif what == "pv":
                                if j == 0:
                                    if s % NT == 0:
                                        pe.wait_ge(v_in[gp], 16 * (k + 1))
                                    pe.wait_ge(o_copied, STEPS * k + s + 1)
                                pe.wait_ge(t_free, TURNS * k + before(s, 1) + j + 1 + TR)
                                for z in range(2):
                                    done = pe.matmul(psum[:, O_BANK, :], v[:, gp, j, :], pt[:, block_no % TR, z, :],
                                                     start=j == 0 and z == 0, stop=j == n - 1 and z == 1)
                                done.then_inc(pv_done, 1)
                            else:
                                pe.wait_ge(o_copied, STEPS * k + s + 2)
                                pe.wait_ge(t_free, TURNS * k + use_before(use) + 1 + TR)
                                for h in range(R):
                                    done = pe.transpose(psum[:, T_BANK + use % TR, h * P:(h + 1) * P],
                                                        o_t[:, s % 2, h * P:(h + 1) * P], const.ident[:, :])
                                done.then_inc(turned, 1)

                with pe.Fori(0, LOOPS - 1) as k:
                    body(k, False)
                body(LOOPS - 1, True)

            @block.scalar
            def _(act):
                def exp(k, s, h):
                    slot, n = s % SLOTS, key_blocks(s)
                    at = slot * R + h
                    src, w = view(psum[:, S_BANKS + 2 * (h % 2):S_BANKS + 2 * (h % 2) + 2, :], n)
                    act.wait_ge(topped, R * (STEPS * k + s) + h + 1)
                    act.activation(probs[:, slot, h, 0:n * P].rearrange("p (a w) -> p a w", w=w), src, ACT.Exp,
                                   bias=top[:, at:at + 1], accum_out=sums[:, at:at + 1]).then_inc(expd, 1)

                for s in range(LEAD):
                    for h in range(R):
                        exp(0, s, h)

                def body(k, last):
                    for s in range(STEPS):
                        dk, s2 = scores_at(s)
                        waiting = []
                        for what, j in order(s, not (last and dk)):
                            if what == "scores":
                                waiting.append(j)
                                if len(waiting) == 2:
                                    exp(k + dk, s2, waiting.pop(0))
                            elif what == "turn":
                                use, no = before(s, 1) + j, before(s, 0) + j
                                act.wait_ge(turned, TURNS * k + use + 1)
                                act.activation(pt[:, no % TR, 0, :], psum[:, T_BANK + use % TR, :], ACT.Copy
                                               ).then_inc(hi_done, 1)
                                for h in waiting:
                                    exp(k + dk, s2, h)
                                waiting = []
                            elif what == "out":
                                act.wait_ge(pv_done, BLOCKS * k + before(s + 1, 0))
                                act.activation(o_t[:, s % 2, :], psum[:, O_BANK, :], ACT.Copy).then_inc(o_copied, 1)

                with act.Fori(0, LOOPS - 1) as k:
                    body(k, False)
                body(LOOPS - 1, True)

            @block.vector
            def _(dve):
                dve.sem_inc(t_free, TR)
                dve.sem_inc(o_copied, 1)
                dve.sem_inc(scaled, 2)
                for i in range(2):
                    dve.sem_inc(stored[i], 1)

                def maximum(k, s, h):
                    at = (s % SLOTS) * R + h
                    src, w = view(psum[:, S_BANKS + 2 * (h % 2):S_BANKS + 2 * (h % 2) + 2, :], key_blocks(s))
                    dve.wait_ge(scored, R * (STEPS * k + s) + h + 1)
                    dve.tensor_reduce(top[:, at:at + 1], src, AX.XY, ALU.max, negate=True).then_inc(topped, 1)

                for s in range(LEAD):
                    for h in range(R):
                        maximum(0, s, h)

                def body(k, last):
                    for s in range(STEPS):
                        dk, s2 = scores_at(s)
                        for what, j in order(s, not (last and dk)):
                            if what == "scores":
                                maximum(k + dk, s2, j)
                            elif what == "turn":
                                use, no = before(s, 1) + j, before(s, 0) + j
                                dve.wait_ge(hi_done, BLOCKS * k + no + 1)
                                dve.tensor_tensor(pt[:, no % TR, 1, :], psum[:, T_BANK + use % TR, :],
                                                  raw(pt[:, no % TR, 0, :]), ALU.subtract).then_inc(t_free, 1)
                            elif what == "out":
                                use = before(s + 1, 1) - 1
                                dve.wait_ge(scaled, STEPS * k + s + 1)
                                dve.wait_ge(expd, R * (STEPS * k + s + 1))
                                dve.reciprocal(inv[:, s % 2, :], sums[:, (s % SLOTS) * R:(s % SLOTS + 1) * R]
                                               ).then_inc(inverted, 1)
                                dve.wait_ge(turned, TURNS * k + use + 1)
                                dve.tensor_copy(o_n[:, s % 2].rearrange("p h d -> p (h d)"),
                                                psum[:, T_BANK + use % TR, :]).then_inc(t_free, 1)

                with dve.Fori(0, LOOPS - 1) as k:
                    body(k, False)
                body(LOOPS - 1, True)

            @block.gpsimd
            def _(pool):
                def body(k):
                    for s in range(STEPS):
                        at = s % 2
                        pool.wait_ge(t_free, TURNS * k + before(s + 1, 1) + TR)
                        pool.tensor_tensor(o_sum[:, at], o_n[:, at, :, 0:HD], o_n[:, at, :, HD:2 * HD], ALU.add
                                           ).then_inc(summed, 1)
                        pool.wait_ge(summed, STEPS * k + s + 1)
                        pool.wait_ge(inverted, STEPS * k + s + 1)
                        pool.wait_ge(stored[at], 16 * (STEPS // 2 * k + s // 2) + 1)
                        pool.tensor_tensor(res[:, at], o_sum[:, at], inv[:, at, :, None].broadcast_to([P, R, HD]), ALU.mult
                                           ).then_inc(scaled, 1)

                with pool.Fori(0, LOOPS) as k:
                    body(k)


def stage_c(nc, dims, dram, const, psum):
    D, G, S, B, E = dims.D, dims.G, dims.S, dims.B, dims.E
    KC = D // P
    TPC = 2
    CH = TPC * P
    NCH = B * S // CH
    LOOPS = NCH // 2
    CPB = S // CH
    NT = 2 * TPC
    XR = 2 * TPC + 2
    UP_BANKS = 2
    WX = D + E
    EB = 3
    EN = WX // EB
    GATE_BANK, GATE_COL = EB - 1, D - (EB - 1) * EN
    assert WX % EB == 0 and EN <= 512 and EN % 2 == 0
    with ExitStack() as c:
        def sb(name, shape, dt=F32):
            return c.enter_context(nc.sbuf_tensor(name, shape, dt))

        def sem(name):
            return c.enter_context(nc.semaphore(name))

        wup = sb("wup_t", [P, 2, KC, D], F32R)
        wex = sb("wex", [P, 2, KC, WX], F32R)
        yt = sb("yt", [P, 2, 2, KC, CH], F32R)
        y = sb("y", [P, 2 * TPC, D])
        att = sb("att_sb", [P, 2, D])
        h_out = sb("h_out", [P, 4, CH])
        w_raw = y
        stats = sb("stats", [P, 2, 2, 6])
        mv = sb("mv", [P, 2 * TPC, 2])
        std = sb("std", [P, 2 * TPC])
        rstd = sb("rstd", [P, 2 * TPC])
        eps = sb("eps_c", [P, 1])
        best = sb("best", [P, 2 * TPC, 8])
        nbest = sb("nbest", [P, 2 * TPC])
        ex = sb("ex", [P, 2 * TPC, 2])
        ex_sum = sb("ex_sum", [P, 2 * TPC])
        ex_inv = sb("ex_inv", [P, 2 * TPC])
        route = sb("route", [P, 2 * TPC, 2])
        route_sum = sb("route_sum", [P, 2 * TPC])
        idle = sem("c_idle")
        w_in = [sem(f"c_w_in{i}") for i in range(4)]
        w_zero = sem("c_w_zero")
        w_turned, w_hi, w_lo = sem("c_w_turned"), sem("c_w_hi"), sem("c_w_lo")
        x_in = [sem(f"c_x_in{i}") for i in range(2 * TPC)]
        att_in = [sem(f"c_att_in{i}") for i in range(2)]
        chain = sem("c_chain")
        var_done, std_done = sem("c_var_done"), sem("c_std_done")
        y_done = sem("c_y_done")
        turned, t_hi, t_lo = sem("c_turned"), sem("c_t_hi"), sem("c_t_lo")
        up_done = sem("c_up_done")
        relu_done = sem("c_relu_done")
        h_stored = [sem(f"c_h_stored{i}") for i in range(4)]
        exp_done_pe = sem("c_expert_done")
        e_free = sem("c_e_free")
        nbest_done, soft_done = sem("c_nbest_done"), sem("c_soft_done")
        r_done = sem("c_r_done")
        r_stored = [sem(f"c_r_stored{i}") for i in range(2 * TPC)]

        EB_ORDER = [GATE_BANK] + [b for b in range(EB) if b != GATE_BANK]
        E_BANK0 = 2 + UP_BANKS

        w_tiles = 2 * KC + 1
        turn_groups = 2 * KC + 2

        with nc.Block() as block:

            @block.sync
            def _(sp):
                for i in range(w_tiles):
                    if i >= 4:
                        j = i - 4
                        if j < KC + 1:
                            sp.wait_ge(w_turned, 2 * (j + 1))
                        else:
                            sp.wait_ge(w_lo, turn_groups + j - KC)
                    dst = w_raw[:, i % 4, :]
                    if i < KC:
                        sp.dma_start(dst, dram.wup[i * P:(i + 1) * P, :]).then_inc(w_in[i % 4], 16)
                    elif i == KC:
                        sp.wait_ge(w_zero, 1)
                        sp.dma_start(dst[0:E, :], dram.wg[:, :]).then_inc(w_in[i % 4], 16)
                    else:
                        e = i - KC - 1
                        sp.dma_start(dst, dram.wex[e * P:(e + 1) * P, :]).then_inc(w_in[i % 4], 16)
                sp.wait_ge(w_lo, turn_groups + KC)

                def load(k, t):
                    tile = 2 * TPC * k + t
                    sp.dma_start(y[:, t, :], dram.x[bass.ds(tile, 1)].rearrange("a p n -> (a p) n")
                                 ).then_inc(x_in[t], 16)
                    sp.dma_start(att[:, t % 2, :], dram.att_tiles[bass.ds(tile, 1)].rearrange("a p n -> (a p) n")
                                 ).then_inc(att_in[t % 2], 16)

                for t in range(2 * TPC):
                    if t >= 2:
                        sp.wait_ge(y_done, t - 1)
                    load(0, t)

                def chunk(k, par, loads):
                    ch = 2 * k + par
                    for n in range(KC):
                        sp.wait_ge(relu_done, KC * ch + n + 1 + UP_BANKS)
                        sp.dma_start(dram.h[bass.ds(TPC * ch, TPC), :, n, :].rearrange("a p t -> p a t"),
                                     h_out[:, n % 4, :].rearrange("p (a t) -> p a t", a=TPC)).then_inc(h_stored[n % 4], 16)
                    for i in range(TPC):
                        t = TPC * par + i
                        sp.wait_ge(e_free, EB * (TPC * ch + i + 1) + EB)
                        sp.dma_start(dram.r[bass.ds(2 * TPC * k + t, 1)].rearrange("a p n -> (a p) n"), y[:, t, :]
                                     ).then_inc(r_stored[t], 16)
                    for i in range(TPC if loads else 0):
                        t = TPC * par + i
                        sp.wait_ge(r_stored[t], 16 * (k + 1))
                        sp.wait_ge(y_done, TPC * (ch + 2))
                        load(k + 1, t)

                with sp.Fori(0, LOOPS - 1) as k:
                    chunk(k, 0, True)
                    chunk(k, 1, True)
                chunk(LOOPS - 1, 0, False)
                chunk(LOOPS - 1, 1, False)
                for i in range(4):
                    sp.wait_ge(h_stored[i], 16 * KC * NCH // 4 + 1)
                for t in range(2 * TPC):
                    sp.wait_ge(r_stored[t], 16 * LOOPS)

            @block.gpsimd
            def _(pool):
                pool.wait_ge(w_turned, 2 * (KC - 4 + 1))
                pool.memset(w_raw[:, KC % 4, :], 0.0).then_inc(w_zero, 1)

            @block.tensor
            def _(pe):
                for n in range(turn_groups):
                    i, half = n // 2, n % 2
                    if half == 0:
                        pe.wait_ge(w_in[i % 4], 16 * (i // 4 + 1))
                    if n >= 2:
                        pe.wait_ge(w_lo, n - 1)
                    for a in range(4):
                        e = 4 * half + a
                        done = pe.transpose(psum[:, n % 2, a * P:(a + 1) * P], w_raw[:, i % 4, e * P:(e + 1) * P],
                                            const.ident[:, :])
                    done.then_inc(w_turned, 1)

                def turn(ch, par, n):
                    i, half = n // 2, n % 2
                    pe.wait_ge(y_done, TPC * ch + i + 1)
                    if isinstance(ch, int) and NT * ch + n < 2:
                        pe.wait_ge(w_lo, turn_groups)
                    else:
                        pe.wait_ge(t_lo, NT * ch + n - 1)
                    for a in range(4):
                        e = 4 * half + a
                        done = pe.transpose(psum[:, n % 2, a * P:(a + 1) * P], y[:, TPC * par + i, e * P:(e + 1) * P],
                                            const.ident[:, :])
                    done.then_inc(turned, 1)

                for n in range(NT):
                    turn(0, 0, n)
                pe.wait_ge(w_lo, turn_groups + KC)
                pe.wait_ge(w_hi, turn_groups + KC)

                def chunk(k, par, more):
                    ch = 2 * k + par
                    pe.wait_ge(t_lo, NT * (ch + 1))
                    for n in range(KC):
                        pe.wait_ge(relu_done, KC * ch + n + 1)
                        for e in range(KC):
                            for zw, zx in ((0, 0), (0, 1), (1, 0)):
                                done = pe.matmul(psum[:, 2 + n % UP_BANKS, 0:CH], wup[:, zw, e, n * P:(n + 1) * P],
                                                 yt[:, par, zx, e, :], start=e == 0 and zw + zx == 0,
                                                 stop=e == KC - 1 and zw == 1)
                        done.then_inc(up_done, 1)
                    for m in range(TPC * EB):
                        i, b = m // EB, EB_ORDER[m % EB]
                        pe.wait_ge(e_free, TPC * EB * ch + m + 1)
                        for e in range(KC):
                            for zw, zx in ((0, 0), (0, 1), (1, 0)):
                                done = pe.matmul(psum[:, E_BANK0 + b, 0:EN], yt[:, par, zx, e, i * P:(i + 1) * P],
                                                 wex[:, zw, e, b * EN:(b + 1) * EN], start=e == 0 and zw + zx == 0,
                                                 stop=e == KC - 1 and zw == 1)
                        done.then_inc(exp_done_pe, 1)
                        if more and 1 <= m <= NT:
                            turn(ch + 1, 1 - par, m - 1)

                with pe.Fori(0, LOOPS - 1) as k:
                    chunk(k, 0, True)
                    chunk(k, 1, True)
                chunk(LOOPS - 1, 0, True)
                chunk(LOOPS - 1, 1, False)

            @block.scalar
            def _(act):
                for n in range(turn_groups):
                    i, half = n // 2, n % 2
                    act.wait_ge(w_turned, n + 1)
                    src = psum[:, n % 2, :].rearrange("p (a t) -> p a t", a=4)
                    dst = wup[:, 0, 4 * half:4 * half + 4, i * P:(i + 1) * P] if i < KC else \
                        wex[:, 0, 4 * half:4 * half + 4, D:WX]
                    act.activation(dst, src if i < KC else src[:, :, 0:E], ACT.Copy).then_inc(w_hi, 1)
                for e in range(KC):
                    i = KC + 1 + e
                    act.wait_ge(w_in[i % 4], 16 * (i // 4 + 1))
                    act.activation(wex[:, 0, e, 0:D], w_raw[:, i % 4, :], ACT.Copy).then_inc(w_hi, 1)

                def root(ch, par):
                    act.wait_ge(var_done, TPC * (ch + 1))
                    act.activation(std[:, TPC * par:TPC * par + TPC], mv[:, TPC * par:TPC * par + TPC, 1], ACT.Sqrt,
                                   bias=eps[:, 0:1]).then_inc(std_done, 1)

                def t_high(ch, par, n):
                    i, half = n // 2, n % 2
                    act.wait_ge(turned, NT * ch + n + 1)
                    act.activation(yt[:, par, 0, 4 * half:4 * half + 4, i * P:(i + 1) * P],
                                   psum[:, n % 2, :].rearrange("p (a t) -> p a t", a=4), ACT.Copy).then_inc(t_hi, 1)

                root(0, 0)
                for n in range(NT):
                    t_high(0, 0, n)

                def chunk(k, par, more):
                    ch = 2 * k + par
                    for n in range(KC):
                        act.wait_ge(up_done, KC * ch + n + 1)
                        act.wait_ge(h_stored[n % 4], 16 * (KC // 4 * ch + n // 4) + 1)
                        act.activation(h_out[:, n % 4, :], psum[:, 2 + n % UP_BANKS, 0:CH], ACT.Relu
                                       ).then_inc(relu_done, 1)
                        if n == 5 and more:
                            root(ch + 1, 1 - par)
                    for m in range(TPC * EB):
                        i, t = m // EB, TPC * par + m // EB
                        if m % EB == 0:
                            act.wait_ge(nbest_done, TPC * ch + i + 1)
                            act.activation(ex[:, t, :], best[:, t, 0:2], ACT.Exp, bias=nbest[:, t:t + 1],
                                           accum_out=ex_sum[:, t:t + 1]).then_inc(soft_done, 1)
                        if more and 1 <= m <= NT:
                            t_high(ch + 1, 1 - par, m - 1)

                with act.Fori(0, LOOPS - 1) as k:
                    chunk(k, 0, True)
                    chunk(k, 1, True)
                chunk(LOOPS - 1, 0, True)
                chunk(LOOPS - 1, 1, False)

            @block.vector
            def _(dve):
                dve.memset(eps[:, :], EPS).then_inc(chain, 1)
                dve.sem_inc(relu_done, UP_BANKS)
                dve.sem_inc(e_free, EB)
                for i in range(4):
                    dve.sem_inc(h_stored[i], 1)
                for n in range(turn_groups):
                    i, half = n // 2, n % 2
                    dve.wait_ge(w_hi, n + 1)
                    src = psum[:, n % 2, :].rearrange("p (a t) -> p a t", a=4)
                    dst = wup[:, :, 4 * half:4 * half + 4, i * P:(i + 1) * P] if i < KC else \
                        wex[:, :, 4 * half:4 * half + 4, D:WX]
                    dve.tensor_tensor(dst[:, 1], src if i < KC else src[:, :, 0:E], raw(dst[:, 0]), ALU.subtract
                                      ).then_inc(w_lo, 1)
                for e in range(KC):
                    dve.wait_ge(w_hi, turn_groups + e + 1)
                    dve.tensor_tensor(wex[:, 1, e, 0:D], w_raw[:, (KC + 1 + e) % 4, :], raw(wex[:, 0, e, 0:D]),
                                      ALU.subtract).then_inc(w_lo, 1)
                LINKS = 7
                STEP = LINKS + 3 * TPC

                def norm(k, ch, par, base):
                    for i in range(TPC):
                        t = TPC * par + i
                        dve.wait_ge(x_in[t], 16 * (k + 1))
                        dve.wait_ge(att_in[t % 2], 16 * (2 * k + t // 2 + 1))
                        dve.tensor_tensor(y[:, t, :], y[:, t, :], att[:, t % 2, :], ALU.add).then_inc(chain, 1)
                    for i in range(TPC):
                        t = TPC * par + i
                        dve.wait_ge(chain, base + i + 1)
                        for half in range(2):
                            dve.bn_stats(stats[:, i, half, :], y[:, t, half * 512:(half + 1) * 512]).then_inc(chain, 1)
                    dve.wait_ge(chain, base + TPC + 2 * TPC)
                    dve.sem_inc(idle, 1)
                    for i in range(TPC):
                        t = TPC * par + i
                        dve.bn_aggr(mv[:, t, :], stats[:, i].rearrange("p a b -> p (a b)")).then_inc(var_done, 1)
                    dve.wait_ge(std_done, ch + 1)
                    dve.reciprocal(rstd[:, TPC * par:TPC * par + TPC], std[:, TPC * par:TPC * par + TPC]
                                   ).then_inc(chain, 1)
                    dve.wait_ge(chain, base + LINKS)
                    for i in range(TPC):
                        t = TPC * par + i
                        dve.tensor_scalar(y[:, t, :], y[:, t, :], mv[:, t, 0:1], rstd[:, t:t + 1], ALU.subtract,
                                          ALU.mult).then_inc(y_done, 1)

                def t_low(ch, par, n):
                    i, half = n // 2, n % 2
                    dve.wait_ge(t_hi, NT * ch + n + 1)
                    at = yt[:, par, :, 4 * half:4 * half + 4, i * P:(i + 1) * P]
                    dve.tensor_tensor(at[:, 1], psum[:, n % 2, :].rearrange("p (a t) -> p a t", a=4), raw(at[:, 0]),
                                      ALU.subtract).then_inc(t_lo, 1)

                norm(0, 0, 0, 1)
                for n in range(NT):
                    t_low(0, 0, n)

                def chunk(k, par, more):
                    ch = 2 * k + par
                    base = 1 + LINKS + STEP * ch
                    if more:
                        norm(k + par, ch + 1, 1 - par, base)
                    base = base + (LINKS if more else 0)
                    for m in range(TPC * EB):
                        i, t, b = m // EB, TPC * par + m // EB, EB_ORDER[m % EB]
                        dve.wait_ge(exp_done_pe, TPC * EB * ch + m + 1)
                        if m % EB == 0:
                            dve.sem_inc(idle, 1)
                            dve.max(best[:, t, :], psum[:, E_BANK0 + b, GATE_COL:GATE_COL + E]).then_inc(chain, 1)
                            dve.wait_ge(chain, base + 3 * i + 1)
                            dve.tensor_scalar(nbest[:, t:t + 1], best[:, t, 0:1], -1.0, None, ALU.mult
                                              ).then_inc(nbest_done, 1)
                            dve.wait_ge(soft_done, TPC * ch + i + 1)
                            dve.reciprocal(ex_inv[:, t:t + 1], ex_sum[:, t:t + 1]).then_inc(chain, 1)
                            dve.wait_ge(chain, base + 3 * i + 2)
                            dve.tensor_scalar(route[:, t, :], ex[:, t, :], ex_inv[:, t:t + 1], 0.0, ALU.mult, ALU.add,
                                              accum_out=route_sum[:, t:t + 1]).then_inc(chain, 1)
                            dve.wait_ge(chain, base + 3 * i + 3)
                        w = EN if b < EB - 1 else GATE_COL
                        cols = slice(b * EN, b * EN + w)
                        dve.scalar_tensor_tensor(y[:, t, cols], psum[:, E_BANK0 + b, 0:w], route_sum[:, t:t + 1],
                                                 y[:, t, cols], op0=ALU.mult, op1=ALU.add).then_inc(e_free, 1)
                        if more and 1 <= m <= NT:
                            t_low(ch + 1, 1 - par, m - 1)

                with dve.Fori(0, LOOPS - 1) as k:
                    chunk(k, 0, True)
                    chunk(k, 1, True)
                chunk(LOOPS - 1, 0, True)
                chunk(LOOPS - 1, 1, False)


def stage_d(nc, dims, dram, const, psum):
    D, S, B = dims.D, dims.S, dims.B
    KC = D // P
    NTILES = B * S // P
    TB = 4
    LOOPS = NTILES // TB
    HALVES, HW = 2, D // 2
    turn_groups = 2 * KC
    with ExitStack() as c:
        def sb(name, shape, dt=F32):
            return c.enter_context(nc.sbuf_tensor(name, shape, dt))

        def sem(name):
            return c.enter_context(nc.semaphore(name))

        wd = sb("wdown_t", [P, 2, KC, D], F32R)
        w_raw = sb("w_raw_d", [P, 4, D])
        h_raw = sb("h_raw", [P, 2, KC, P])
        ht = sb("ht", [P, 2, 2, KC, P], F32R)
        r = sb("r_sb", [P, TB, D])
        stats = sb("stats_d", [P, 2, HALVES, 6])
        mv = sb("mv_d", [P, 2, 2])
        std = sb("std_d", [P, 2])
        rstd = sb("rstd_d", [P, 2])
        eps = sb("eps_d", [P, 1])
        idle = sem("d_idle")
        w_in = [sem(f"d_w_in{i}") for i in range(4)]
        w_turned, w_hi, w_lo = sem("d_w_turned"), sem("d_w_hi"), sem("d_w_lo")
        h_in = [sem(f"d_h_in{i}") for i in range(2)]
        r_in = [sem(f"d_r_in{i}") for i in range(TB)]
        h_hi, h_lo = sem("d_h_hi"), sem("d_h_lo")
        done_half = sem("d_done_half")
        added = sem("d_added")
        counted, var_done, std_done, inverted = sem("d_counted"), sem("d_var_done"), sem("d_std_done"), sem("d_inverted")
        normed = sem("d_normed")
        eps_set = sem("d_eps_set")
        stored = [sem(f"d_stored{i}") for i in range(TB)]
        BANK0 = 2

        with nc.Block() as block:

            @block.sync
            def _(sp):
                def load_h(tile, par):
                    sp.dma_start(h_raw[:, par], dram.h[bass.ds(tile, 1)].rearrange("a p n t -> (a p) n t")
                                 ).then_inc(h_in[par], 16)

                def load_r(tile, t):
                    sp.dma_start(r[:, t, :], dram.r[bass.ds(tile, 1)].rearrange("a p n -> (a p) n")
                                 ).then_inc(r_in[t], 16)

                for i in range(KC):
                    if i >= 4:
                        sp.wait_ge(w_turned, 2 * (i - 3))
                    sp.dma_start(w_raw[:, i % 4, :], dram.wdown[i * P:(i + 1) * P, :]).then_inc(w_in[i % 4], 16)
                for t in range(2):
                    load_h(t, t)
                for t in range(TB - 1):
                    load_r(t, t)
                sp.wait_ge(h_lo, 1)
                load_h(2, 0)

                def step(k, t, more_h, more_r, first):
                    if more_h:
                        sp.wait_ge(h_lo, TB * k + t + 2)
                        load_h(TB * k + t + 3, (t + 1) % 2)
                    sp.wait_ge(normed, TB * k + t + 1)
                    sp.dma_start(dram.out[bass.ds(TB * k + t, 1)].rearrange("a p n -> (a p) n"), r[:, t, :]
                                 ).then_inc(stored[t], 16)
                    if more_r:
                        if t >= 1:
                            sp.wait_ge(stored[t - 1], 16 * (k + 1))
                        elif not first:
                            sp.wait_ge(stored[TB - 1], 16 * k)
                        load_r(TB * k + t + TB - 1, (t + TB - 1) % TB)

                for t in range(TB):
                    step(0, t, True, True, True)
                with sp.Fori(1, LOOPS - 1) as k:
                    for t in range(TB):
                        step(k, t, True, True, False)
                for t in range(TB):
                    step(LOOPS - 1, t, t + 3 < TB, t + TB - 1 < TB, False)
                for t in range(TB):
                    sp.wait_ge(stored[t], 16 * LOOPS)

            @block.tensor
            def _(pe):
                for n in range(turn_groups):
                    i, half = n // 2, n % 2
                    if half == 0:
                        pe.wait_ge(w_in[i % 4], 16 * (i // 4 + 1))
                    if n >= 2:
                        pe.wait_ge(w_lo, n - 1)
                    for a in range(4):
                        e = 4 * half + a
                        done = pe.transpose(psum[:, n % 2, a * P:(a + 1) * P], w_raw[:, i % 4, e * P:(e + 1) * P],
                                            const.ident[:, :])
                    done.then_inc(w_turned, 1)
                pe.wait_ge(w_lo, turn_groups)
                with pe.Fori(0, LOOPS) as k:
                    for t in range(TB):
                        par = t % 2
                        pe.wait_ge(h_lo, TB * k + t + 1)
                        for half in range(HALVES):
                            bank = BANK0 + HALVES * par + half
                            pe.wait_ge(added, HALVES * (TB * k + t) + half + 1)
                            for e in range(KC):
                                for zh, zw in ((0, 0), (0, 1), (1, 0)):
                                    done = pe.matmul(psum[:, bank, :], ht[:, par, zh, e, :],
                                                     wd[:, zw, e, half * HW:(half + 1) * HW],
                                                     start=e == 0 and zh + zw == 0, stop=e == KC - 1 and zh == 1)
                            done.then_inc(done_half, 1)

            @block.scalar
            def _(act):
                for n in range(turn_groups):
                    i, half = n // 2, n % 2
                    act.wait_ge(w_turned, n + 1)
                    act.activation(wd[:, 0, 4 * half:4 * half + 4, i * P:(i + 1) * P],
                                   psum[:, n % 2, :].rearrange("p (a t) -> p a t", a=4), ACT.Copy).then_inc(w_hi, 1)

                def high(k, t):
                    act.wait_ge(h_in[t % 2], 16 * (TB // 2 * k + t // 2 + 1))
                    if not (isinstance(k, int) and TB * k + t < 2):
                        act.wait_ge(done_half, HALVES * (TB * k + t - 1))
                    act.activation(ht[:, t % 2, 0], h_raw[:, t % 2], ACT.Copy).then_inc(h_hi, 1)

                def step(k, t, more):
                    if more:
                        high(k + (t + 1) // TB, (t + 1) % TB)
                    act.wait_ge(var_done, TB * k + t + 1)
                    act.activation(std[:, t % 2:t % 2 + 1], mv[:, t % 2, 1:2], ACT.Sqrt, bias=eps[:, 0:1]
                                   ).then_inc(std_done, 1)

                act.wait_ge(eps_set, 1)
                high(0, 0)
                for t in range(TB):
                    step(0, t, True)
                with act.Fori(1, LOOPS - 1) as k:
                    for t in range(TB):
                        step(k, t, True)
                for t in range(TB):
                    step(LOOPS - 1, t, t + 1 < TB)

            @block.vector
            def _(dve):
                dve.memset(eps[:, :], EPS).then_inc(eps_set, 1)
                dve.sem_inc(added, 2 * HALVES)
                for n in range(turn_groups):
                    i, half = n // 2, n % 2
                    dve.wait_ge(w_hi, n + 1)
                    at = wd[:, :, 4 * half:4 * half + 4, i * P:(i + 1) * P]
                    dve.tensor_tensor(at[:, 1], psum[:, n % 2, :].rearrange("p (a t) -> p a t", a=4), raw(at[:, 0]),
                                      ALU.subtract).then_inc(w_lo, 1)

                def low(k, t):
                    dve.wait_ge(h_hi, TB * k + t + 1)
                    dve.tensor_tensor(ht[:, t % 2, 1], h_raw[:, t % 2], raw(ht[:, t % 2, 0]), ALU.subtract
                                      ).then_inc(h_lo, 1)

                def step(k, t, more):
                    if more:
                        low(k + (t + 1) // TB, (t + 1) % TB)
                    par, tile = t % 2, TB * k + t
                    dve.wait_ge(r_in[t], 16 * (k + 1))
                    for half in range(HALVES):
                        cols = slice(half * HW, (half + 1) * HW)
                        dve.wait_ge(done_half, HALVES * tile + half + 1)
                        dve.tensor_tensor(r[:, t, cols], psum[:, BANK0 + HALVES * par + half, :], r[:, t, cols], ALU.add
                                          ).then_inc(added, 1)
                        dve.wait_ge(added, HALVES * tile + half + 1 + 2 * HALVES)
                        dve.bn_stats(stats[:, par, half, :], r[:, t, cols]).then_inc(counted, 1)
                    dve.wait_ge(counted, HALVES * (tile + 1))
                    dve.sem_inc(idle, 1)
                    dve.bn_aggr(mv[:, par, :], stats[:, par].rearrange("p a b -> p (a b)")).then_inc(var_done, 1)
                    dve.wait_ge(std_done, tile + 1)
                    dve.reciprocal(rstd[:, par:par + 1], std[:, par:par + 1]).then_inc(inverted, 1)
                    dve.wait_ge(inverted, tile + 1)
                    dve.tensor_scalar(r[:, t, :], r[:, t, :], mv[:, par, 0:1], rstd[:, par:par + 1], ALU.subtract,
                                      ALU.mult).then_inc(normed, 1)

                low(0, 0)
                with dve.Fori(0, LOOPS - 1) as k:
                    for t in range(TB):
                        step(k, t, True)
                for t in range(TB):
                    step(LOOPS - 1, t, t + 1 < TB)


def post_ln_layer(nc, x, wq, bq, wk, bk, wv, bv, wup, wdown, wg, wex, out):
    dims, dram, const = Names(), Names(), Names()
    dims.B, dims.S, dims.D = x.shape
    dims.H, _, dims.HD = wq.shape
    dims.G = wk.shape[0]
    dims.E = wg.shape[0]
    B, S, D, H, G, HD = dims.B, dims.S, dims.D, dims.H, dims.G, dims.HD

    def scratch(name, *shape):
        return nc.dram_tensor(name, shape, F32, kind="Internal").ap()

    dram.x = x.rearrange("b (i p) n -> (b i) p n", p=P)
    dram.out = out.rearrange("b (i p) n -> (b i) p n", p=P)
    dram.wq, dram.wk, dram.wv = wq, wk, wv
    dram.bq = bq.rearrange("h (d a) -> (h d) a", a=1)
    dram.bk = bk.rearrange("g (d a) -> (g d) a", a=1)
    dram.bv = bv.rearrange("(a g) d -> a (g d)", a=1)
    dram.wup, dram.wdown, dram.wg, dram.wex = wup, wdown, wg, wex
    dram.q = scratch("q_split", B * G, H // G, 2 * HD, S)
    dram.k = scratch("k_split", B * G, 2, HD, S)
    dram.v = scratch("v_split", B * G, S, 2 * HD)
    dram.att = scratch("attention", B, S, G, H // G * HD)
    dram.att_tiles = dram.att.rearrange("b (i p) g n -> (b i) p (g n)", p=P)
    dram.h = scratch("hidden_t", B * S // P, P, D // P, P)
    dram.r = scratch("residual", B * S // P, P, D)

    with ExitStack() as c:
        psum_t = c.enter_context(nc.psum_tensor("banks", [P, 8, 512], F32))
        const.ident = c.enter_context(nc.sbuf_tensor("ident", [P, P], F32))
        const.ident_bf = c.enter_context(nc.sbuf_tensor("ident_bf", [P, P], BF16))
        const.mask = c.enter_context(nc.sbuf_tensor("mask", [P, P], BF16))
        constants(nc, c, const)
        stage_a(nc, dims, dram, const, psum_t)
        stage_b(nc, dims, dram, const, psum_t)
        stage_c(nc, dims, dram, const, psum_t)
        stage_d(nc, dims, dram, const, psum_t)


_INS = ["L0_attn_x", "L0_attn_Wq", "L0_attn_bq", "L0_attn_Wk", "L0_attn_bk", "L0_attn_Wv", "L0_attn_bv",
        "L0_ffn_W_up", "L0_ffn_W_down", "L0_ffn_W_gate", "L0_ffn_W_expert"]


def kernel(**inputs):
    import numpy as _np
    import concourse.bacc as _bacc
    from concourse import mybir as _mybir
    from concourse.bass_utils import run_bass_kernel_spmd as _run

    nc = _bacc.Bacc("TRN2", target_bir_lowering=False, num_devices=1)
    arrays, args = {}, []
    for name in _INS:
        a = _np.ascontiguousarray(inputs[name])
        arrays[f"in_{name}"] = a
        args.append(nc.dram_tensor(f"in_{name}", a.shape, _mybir.dt.from_np(a.dtype), kind="ExternalInput").ap())
    shape = arrays["in_L0_attn_x"].shape
    args.append(nc.dram_tensor("out_dram", shape, _mybir.dt.float32, kind="ExternalOutput").ap())
    post_ln_layer(nc, *args)
    r = _run(nc, [arrays], core_ids=[0])
    return r.results[0]["out_dram"]
```

```python
from contextlib import ExitStack

import numpy as np

import concourse.bass as bass
from concourse import mybir
from concourse.alu_op_type import AluOpType as ALU

F32 = mybir.dt.float32
F32R = mybir.dt.float32r
BF16 = mybir.dt.bfloat16
ACT = mybir.ActivationFunctionType
AX = mybir.AxisListType
P = 128
EPS = 1e-5
MASKED = -3.0e38


class Names:
    pass


def raw(ap):
    return ap.bitcast(F32)


def constants(nc, const):
    with ExitStack() as c:
        mask_f = c.enter_context(nc.sbuf_tensor("mask_f", [P, P], F32))
        made = c.enter_context(nc.semaphore("constants_made"))
        rounded = c.enter_context(nc.semaphore("constants_rounded"))
        with nc.Block() as block:

            @block.gpsimd
            def _(pool):
                pool.memset(const.ident[:, :], 0.0).then_inc(made, 1)
                pool.memset(mask_f[:, :], 0.0).then_inc(made, 1)
                pool.wait_ge(made, 2)
                pool.affine_select(out=const.ident[:, :], in_=const.ident[:, :], compare_op=ALU.not_equal, fill=1.0,
                                   base=0, pattern=[[-1, P]], channel_multiplier=1).then_inc(made, 1)
                pool.affine_select(out=mask_f[:, :], in_=mask_f[:, :], compare_op=ALU.is_ge, fill=MASKED, base=0,
                                   pattern=[[-1, P]], channel_multiplier=1).then_inc(made, 1)

            @block.vector
            def _(dve):
                dve.wait_ge(made, 4)
                dve.tensor_copy(const.ident_r[:, :], const.ident[:, :]).then_inc(rounded, 1)
                dve.tensor_copy(const.mask[:, :], mask_f[:, :]).then_inc(rounded, 1)
                half = const.fold.shape[1]
                dve.tensor_tensor(const.fold[:, :], const.ident[:, 0:half], const.ident[:, half:2 * half], ALU.add
                                  ).then_inc(rounded, 1)
                dve.wait_ge(rounded, 3)


def stage_a(nc, dims, dram, const, psum):
    D, H, G, HD, S, B = dims.D, dims.H, dims.G, dims.HD, dims.S, dims.B
    KC = D // P
    CH = 512
    TPC = CH // P
    NQ, NK = H * HD // P, G * HD // P
    NQK = NQ + NK
    NG = NQK + TPC
    NT = 2 * TPC
    KV = G * HD
    RING, SLOTS = 4, 4
    SCALE = 1.0 / float(np.sqrt(HD))
    with ExitStack() as c:
        def sb(name, shape, dt=F32):
            return c.enter_context(nc.sbuf_tensor(name, shape, dt))

        def sem(name):
            return c.enter_context(nc.semaphore(name))

        wq = sb("wq", [P, 2, KC, D], F32R)
        wk = sb("wk", [P, 2, KC, KV], F32R)
        wv = sb("wv", [P, 2, KC, KV], F32R)
        xt = sb("xt", [P, 2, 2, KC, CH], F32R)
        x_raw = sb("x_raw", [P, 2, D])
        w_raw = sb("w_raw", [P, 2, D])
        stage = sb("stage", [P, SLOTS, 2, CH], F32R)
        v_sum = sb("v_sum", [P, 2, KV])
        v_out = sb("v_out", [P, 2, G, 2, HD], F32R)
        bias = sb("bias", [P, NQK])
        bias_s = sb("bias_s", [P, NQK])
        bias_v = sb("bias_v", [P, KV])
        x_in = [sem(f"a_x_in{i}") for i in range(2)]
        w_in = [sem(f"a_w_in{i}") for i in range(2)]
        bias_in = sem("a_bias_in")
        bias_scaled = sem("a_bias_scaled")
        w_hi, w_lo = sem("a_w_hi"), sem("a_w_lo")
        t_done, t_hi, t_lo = sem("a_t_done"), sem("a_t_hi"), sem("a_t_lo")
        group_done = sem("a_group_done")
        qk_hi = sem("a_qk_hi")
        drained = sem("a_drained")
        stored = [sem(f"a_stored{i}") for i in range(SLOTS)]
        v_hi = sem("a_v_hi")
        v_lo = sem("a_v_lo")
        v_stored = [sem(f"a_v_stored{i}") for i in range(2)]

        NCH = B * S // CH
        x_tiles = dram.x
        w_pieces = KC + KC // 2

        def piece(i):
            src = w_raw[:, i % 2, :]
            if i < KC:
                return [(wq[:, 0, i, :], wq[:, 1, i, :], src, SCALE)]
            j = i - KC
            v = src.rearrange("p (a s n) -> p a s n", a=2, s=2)
            return [(w[:, 0, 2 * j:2 * j + 2, :], w[:, 1, 2 * j:2 * j + 2, :], v[:, a], 1.0)
                    for a, w in enumerate((wk, wv))]

        with nc.Block() as block:

            @block.sync
            def _(sp):
                def load_x(tile, slot):
                    sp.dma_start(x_raw[:, slot, :],
                                 x_tiles[bass.ds(tile, 1), :, :].rearrange("a p n -> (a p) n")
                                 ).then_inc(x_in[slot], 16)

                load_x(0, 0)
                load_x(1, 1)
                for i in range(2, 6):
                    sp.wait_ge(t_done, 2 * (i - 1))
                    load_x(i, i % 2)

                def chunk(k, par, t_next, x_next):
                    ch = 2 * k + par
                    for n in range(NQK):
                        m = NQK * par + n
                        slot = m % SLOTS
                        sp.wait_ge(drained, 2 * NG * k + NG * par + n + 1 + RING)
                        for z in range(2):
                            if n < NQ:
                                g, hh = n // 2, 2 * (n % 2)
                                dst = dram.q[bass.ds(k * G + g, 1), hh:hh + 2, z * HD:(z + 1) * HD,
                                             par * CH:(par + 1) * CH].rearrange("a h d t -> (a h) d t")
                            else:
                                dst = dram.k[bass.ds(k * G + 2 * (n - NQ), 2), z, :, par * CH:(par + 1) * CH]
                            sp.dma_start(dst, raw(stage[:, slot, z, :])).then_inc(stored[slot], 16)
                        i = n // 2 + 2
                        if n % 2 == 1 and n < NT and (t_next if i < TPC else x_next):
                            sp.wait_ge(t_done, NT * ch + NT + n + 1)
                            load_x(TPC * ch + TPC + i, i % 2)
                    for i in range(TPC):
                        m = TPC * par + i
                        sp.wait_ge(v_lo, 2 * TPC * k + m + 1 + 2)
                        dst = dram.v[bass.ds(k * G, G), (TPC * par + i) * P:(TPC * par + i + 1) * P, :]
                        sp.dma_start(dst.rearrange("g t f -> t g f"),
                                     raw(v_out[:, i % 2]).rearrange("p g z d -> p g (z d)")
                                     ).then_inc(v_stored[i % 2], 16)

                with sp.Fori(0, NCH // 2 - 1) as k:
                    chunk(k, 0, True, True)
                    chunk(k, 1, True, True)
                k = NCH // 2 - 1
                chunk(k, 0, True, False)
                chunk(k, 1, False, False)
                for s in range(SLOTS):
                    sp.wait_ge(stored[s], 32 * NQK * NCH // SLOTS + 1)
                for s in range(2):
                    sp.wait_ge(v_stored[s], 16 * TPC * NCH // 2 + 1)

            @block.scalar
            def _(act):
                for m in range(NQ):
                    act.dma_start(bias[:, m:m + 1], dram.bq[m * P:(m + 1) * P, :]).then_inc(bias_in, 16)
                for m in range(NK):
                    act.dma_start(bias[:, NQ + m:NQ + m + 1], dram.bk[m * P:(m + 1) * P, :]).then_inc(bias_in, 16)
                act.dma_start(bias_v[:, :], dram.bv.broadcast_to([P, KV])).then_inc(bias_in, 16)

                def load_w(i):
                    dst = w_raw[:, i % 2, :]
                    if i < KC:
                        act.dma_start(dst.rearrange("p (h d) -> p h d", d=HD),
                                      dram.wq[:, i * P:(i + 1) * P, :].rearrange("h p d -> p h d")
                                      ).then_inc(w_in[i % 2], 16)
                        return
                    j = i - KC
                    for a, w in enumerate((dram.wk, dram.wv)):
                        for s in range(2):
                            e = (2 * j + s) * P
                            act.dma_start(dst[:, (2 * a + s) * KV:(2 * a + s + 1) * KV].rearrange("p (g d) -> p g d", d=HD),
                                          w[:, e:e + P, :].rearrange("g p d -> p g d")).then_inc(w_in[i % 2], 16)

                load_w(0)
                load_w(1)

                def t_high(n, par, count):
                    act.wait_ge(t_done, count + 1)
                    act.activation(xt[:, par, 0, 4 * (n % 2):4 * (n % 2) + 4, (n // 2) * P:(n // 2 + 1) * P],
                                   psum[:, n % 2, :].rearrange("p (a t) -> p a t", a=4), ACT.Copy).then_inc(t_hi, 1)

                for n in range(NT):
                    t_high(n, 0, n)
                arrived = [0, 0]
                for i in range(w_pieces):
                    arrived[i % 2] += 16 if i < KC else 64
                    act.wait_ge(w_in[i % 2], arrived[i % 2])
                    for hi, lo, src, scale in piece(i):
                        done = act.activation(hi, src, ACT.Copy, scale=scale)
                    done.then_inc(w_hi, 1)
                    if i + 2 < w_pieces:
                        act.wait_ge(w_lo, i + 1)
                        act.wait_ge(w_hi, i + 1)
                        load_w(i + 2)
                act.wait_ge(bias_scaled, 1)

                def chunk(k, par, t_next):
                    ch = 2 * k + par
                    for n in range(NG):
                        bank = 2 + (NG * par + n) % RING
                        if n < NQK:
                            m = NQK * par + n
                            act.wait_ge(group_done, 2 * NG * k + NG * par + n + 1)
                            act.wait_ge(stored[m % SLOTS], 2 * NQK // SLOTS * 32 * k + 32 * (m // SLOTS) + 1)
                            act.activation(stage[:, m % SLOTS, 0, :], psum[:, bank, :], ACT.Identity,
                                           bias=bias_s[:, n:n + 1]).then_inc(qk_hi, 1)
                        else:
                            i = n - NQK
                            m = TPC * par + i
                            act.wait_ge(drained, 2 * NG * k + NG * par + n + 1 + RING)
                            act.wait_ge(v_stored[i % 2], 16 * (TPC * k + m // 2) + 1)
                            act.activation(v_out[:, i % 2, :, 0, :],
                                           v_sum[:, i % 2, :].rearrange("p (g d) -> p g d", d=HD),
                                           ACT.Copy).then_inc(v_hi, 1)
                        if n < NT and t_next:
                            t_high(n, 1 - par, NT * ch + NT + n)

                with act.Fori(0, NCH // 2 - 1) as k:
                    chunk(k, 0, True)
                    chunk(k, 1, True)
                chunk(NCH // 2 - 1, 0, True)
                chunk(NCH // 2 - 1, 1, False)

            @block.vector
            def _(dve):
                dve.sem_inc(drained, RING)
                for s in range(SLOTS):
                    dve.sem_inc(stored[s], 1)
                for s in range(2):
                    dve.sem_inc(v_stored[s], 1)
                dve.sem_inc(v_lo, 2)

                def t_low(n, par, count):
                    dve.wait_ge(t_hi, count + 1)
                    cols = (slice(4 * (n % 2), 4 * (n % 2) + 4), slice((n // 2) * P, (n // 2 + 1) * P))
                    dve.tensor_tensor(xt[:, par, 1, cols[0], cols[1]],
                                      psum[:, n % 2, :].rearrange("p (a t) -> p a t", a=4),
                                      raw(xt[:, par, 0, cols[0], cols[1]]), ALU.subtract).then_inc(t_lo, 1)

                for n in range(NT):
                    t_low(n, 0, n)
                for i in range(w_pieces):
                    dve.wait_ge(w_hi, i + 1)
                    for hi, lo, src, scale in piece(i):
                        done = dve.scalar_tensor_tensor(lo, src, scale, raw(hi), op0=ALU.mult, op1=ALU.subtract)
                    done.then_inc(w_lo, 1)
                dve.wait_ge(bias_in, 16 * (NQK + 1))
                dve.tensor_scalar(bias_s[:, 0:NQ], bias[:, 0:NQ], SCALE, None, ALU.mult)
                dve.tensor_copy(bias_s[:, NQ:NQK], bias[:, NQ:NQK]).then_inc(bias_scaled, 1)
                dve.wait_ge(bias_scaled, 1)

                def chunk(k, par, t_next):
                    ch = 2 * k + par
                    for n in range(NG):
                        bank = 2 + (NG * par + n) % RING
                        if n < NQK:
                            m = NQK * par + n
                            dve.wait_ge(qk_hi, 2 * NQK * k + m + 1)
                            dve.scalar_tensor_tensor(stage[:, m % SLOTS, 1, :], psum[:, bank, :], bias_s[:, n:n + 1],
                                                     raw(stage[:, m % SLOTS, 0, :]), op0=ALU.add,
                                                     op1=ALU.subtract).then_inc(drained, 1)
                        else:
                            i = n - NQK
                            m = TPC * par + i
                            dve.wait_ge(group_done, 2 * NG * k + NG * par + n + 1)
                            dve.wait_ge(v_lo, 2 * TPC * k + m + 1)
                            dve.tensor_tensor(v_sum[:, i % 2, :], psum[:, bank, 0:KV], bias_v[:, :],
                                              ALU.add).then_inc(drained, 1)
                        if n < NT and t_next:
                            t_low(n, 1 - par, NT * ch + NT + n)

                with dve.Fori(0, NCH // 2 - 1) as k:
                    chunk(k, 0, True)
                    chunk(k, 1, True)
                chunk(NCH // 2 - 1, 0, True)
                chunk(NCH // 2 - 1, 1, False)

            @block.gpsimd
            def _(pool):
                with pool.Fori(0, NCH) as ch:
                    for i in range(TPC):
                        pool.wait_ge(v_hi, TPC * ch + i + 1)
                        pool.tensor_tensor(v_out[:, i % 2, :, 1, :],
                                           v_sum[:, i % 2, :].rearrange("p (g d) -> p g d", d=HD),
                                           raw(v_out[:, i % 2, :, 0, :]), ALU.subtract).then_inc(v_lo, 1)

            @block.tensor
            def _(pe):
                def turn(n, ch):
                    i = n // 2
                    if n % 2 == 0:
                        pe.wait_ge(x_in[i % 2], 16 * (TPC // 2 * ch + i // 2 + 1))
                    if not (isinstance(ch, int) and NT * ch + n < 2):
                        pe.wait_ge(t_lo, NT * ch + n - 1)
                    for a in range(4):
                        e = 4 * (n % 2) + a
                        done = pe.transpose(psum[:, n % 2, a * P:(a + 1) * P], x_raw[:, i % 2, e * P:(e + 1) * P],
                                            const.ident[:, :])
                    done.then_inc(t_done, 1)

                for n in range(NT):
                    turn(n, 0)
                pe.wait_ge(w_lo, w_pieces)
                pe.wait_ge(w_hi, w_pieces)

                def chunk(k, par, t_next):
                    ch = 2 * k + par
                    pe.wait_ge(t_lo, NT * ch + NT)
                    for n in range(NG):
                        bank = 2 + (NG * par + n) % RING
                        pe.wait_ge(drained, 2 * NG * k + NG * par + n + 1)
                        for e in range(KC):
                            for zw, zx in ((0, 0), (0, 1), (1, 0)):
                                first, last = e == 0 and zw + zx == 0, e == KC - 1 and zw == 1
                                if n < NQ:
                                    out, lhs, rhs = psum[:, bank, :], wq[:, zw, e, n * P:(n + 1) * P], xt[:, par, zx, e, :]
                                elif n < NQK:
                                    o = (n - NQ) * P
                                    out, lhs, rhs = psum[:, bank, :], wk[:, zw, e, o:o + P], xt[:, par, zx, e, :]
                                else:
                                    o = (n - NQK) * P
                                    out, lhs, rhs = psum[:, bank, 0:KV], xt[:, par, zx, e, o:o + P], wv[:, zw, e, :]
                                done = pe.matmul(out, lhs, rhs, start=first, stop=last)
                        done.then_inc(group_done, 1)
                        if n < NT and t_next:
                            turn(n, ch + 1)

                with pe.Fori(0, NCH // 2 - 1) as k:
                    chunk(k, 0, True)
                    chunk(k, 1, True)
                chunk(NCH // 2 - 1, 0, True)
                chunk(NCH // 2 - 1, 1, False)


def stage_b(nc, dims, dram, const, psum):
    G, HD, S, B = dims.G, dims.HD, dims.S, dims.B
    R = dims.H // G
    NT = S // P
    STEPS = 2 * NT
    ROWS = STEPS * R
    BLOCKS = NT * (NT + 1)
    ROW_LEAD, TURN_LEAD, PV_LEAD = 16, 5, 2
    PART_COST = 256
    PTR = 4
    S_BANKS, T_BANK, O_BANK = 4, 4, 6
    LOOPS = B * G // 2
    PROBS = BLOCKS // 2
    TILES = [t for i in range(NT // 2) for t in (i, NT - 1 - i)]
    assert R * P == 512 and BLOCKS % PTR == 0 and PTR > TURN_LEAD - PV_LEAD and PV_LEAD >= 2

    def tile_of(step):
        return TILES[step % NT]

    def key_blocks(step):
        return tile_of(step) + 1

    def first_block(step):
        return step // STEPS * BLOCKS + sum(key_blocks(t) for t in range(step % STEPS))

    def step_of(block):
        return next(t for t in range(block // BLOCKS * STEPS, (block // BLOCKS + 1) * STEPS)
                    if first_block(t) <= block < first_block(t + 1))

    def row_banks(row):
        def banks(r):
            return 1 if key_blocks(r // R) * P <= 512 else 2
        return sum(banks(r) for r in range(row % ROWS)) % S_BANKS, banks(row)

    def row_before(row, part):
        at = row_banks(row)[0] + part
        r = row - 1
        while at not in range(row_banks(r % ROWS)[0], sum(row_banks(r % ROWS))):
            r -= 1
        return r

    def group_parts():
        parts = [(row, part) for row in range(R * NT) for part in range(row_banks(row)[1])]
        costs = [key_blocks(row // R) * P // row_banks(row)[1] + PART_COST for row, _ in parts]
        ends = {}
        for group in range(2):
            out, last = [], 0
            for n, (row, part) in enumerate(parts):
                before = ends.get(R * NT * group + row_before(R * NT + row, part) - R * NT, -ROW_LEAD)
                last = max(last, before + 2, BLOCKS // 2 * group + sum(costs[:n]) * (BLOCKS // 2) // sum(costs))
                ends[R * NT * group + row] = last
                out.append((row, part, last - BLOCKS // 2 * group))
        return out

    def parts_at(i):
        return [(R * NT * g + row, part) for g in range(3) for row, part, at in GROUP_PARTS
                if BLOCKS // 2 * g + at - ROW_LEAD == i]

    GROUP_PARTS = group_parts()
    assert all(at - ROW_LEAD + 2 <= first_block(row // R) - TURN_LEAD for row, _, at in GROUP_PARTS)
    PARTS_AT = {i: parts_at(i) for i in range(-ROW_LEAD, BLOCKS)}

    def ends_row(row, part):
        return part == row_banks(row)[1] - 1

    def exps_at(i):
        early, rest = [], []
        for row, part in PARTS_AT.get(i, []):
            while rest and rest[0] <= row_before(row, part):
                early.append(rest.pop(0))
            if ends_row(row, part):
                rest.append(row)
        return early, rest

    def positions(part):
        for i in range(-ROW_LEAD, 0) if part == "prologue" else range(BLOCKS):
            end = 1 if part == "last" else 2
            parts = [(r, p) for r, p in PARTS_AT[i] if r < end * ROWS]
            turn, pv = (x if 0 <= x < end * BLOCKS else None for x in (i + TURN_LEAD, i + PV_LEAD))
            copy = [s for s in range(end * STEPS) if first_block(s + 1) - 2 == i]
            out = [s for s in range(end * STEPS) if min(first_block(s + 1), first_block(s + 2) - PV_LEAD) == i]
            yield i, parts, turn, pv, copy, out

    with ExitStack() as c:
        def sb(name, shape, dt=F32):
            return c.enter_context(nc.sbuf_tensor(name, shape, dt))

        def sem(name):
            return c.enter_context(nc.semaphore(name))

        q = sb("q_sb", [P, 2, R, S], F32R)
        kk = sb("k_sb", [P, 2, 2, S], F32R)
        v = sb("v_sb", [P, 2, NT, 2 * HD], F32R)
        probs = sb("probs", [P, PROBS * R * P])
        pt = sb("pt", [P, PTR, 2, R * P], F32R)
        top = sb("top", [P, ROWS])
        sums = sb("sums", [P, ROWS])
        inv = sb("inv", [P, 2, R])
        o_t = sb("o_t", [P, 2, R * P])
        res = sb("res", [P, 2, R, HD])
        qk_in = [sem(f"b_qk_in{i}") for i in range(2)]
        v_in = [sem(f"b_v_in{i}") for i in range(2)]
        scored, topped, expd = sem("b_scored"), sem("b_topped"), sem("b_expd")
        turned, hi_done, lo_done = sem("b_turned"), sem("b_hi_done"), sem("b_lo_done")
        pv_done = sem("b_pv_done")
        o_copied, o_turned, inverted = sem("b_o_copied"), sem("b_o_turned"), sem("b_inverted")
        scaled = sem("b_scaled")
        stored = [sem(f"b_stored{i}") for i in range(2)]
        idle = sem("b_idle")

        def row_probs(s, h):
            n = key_blocks(s)
            at = (first_block(s) % PROBS * R + h * n) * P
            return probs[:, at:at + n * P]

        def row_view(ap, n):
            banks = 1 if n * P <= 512 else 2
            return ap[:, :, 0:n * P // banks]

        with nc.Block() as block:

            @block.sync
            def _(sp):
                def load_qk(g, par):
                    sp.dma_start(raw(q[:, par]), dram.q[bass.ds(g, 1)].rearrange("a h p t -> (a p) h t")
                                 ).then_inc(qk_in[par], 16)
                    for half in range(2):
                        sp.dma_start(raw(kk[half * HD:(half + 1) * HD, par]),
                                     dram.k[bass.ds(g, 1)].rearrange("a z p t -> (a p) z t")).then_inc(qk_in[par], 16)

                def load_v(g, par):
                    sp.dma_start(raw(v[:, par]), dram.v[bass.ds(g, 1)].rearrange("a (j p) f -> p (a j) f", p=P)
                                 ).then_inc(v_in[par], 16)

                for g in range(2):
                    load_qk(g, g)
                    load_v(g, g)

                def body(k, last):
                    for s in range(STEPS):
                        gp, tile = s // NT, tile_of(s)
                        sp.wait_ge(scaled, STEPS * k + s + 1 + 2)
                        sp.sem_inc(idle, 1)
                        sp.dma_start(dram.att[bass.ds(k // (G // 2), 1), tile * P:(tile + 1) * P,
                                              bass.ds(2 * (k % (G // 2)) + gp, 1), :].rearrange("a t g n -> t (a g n)"),
                                     res[:, s % 2].rearrange("p h d -> p (h d)")).then_inc(stored[s % 2], 16)
                        if last:
                            continue
                        if s in (NT - 3, STEPS - 3):
                            sp.wait_ge(scored, ROWS * k + R * NT * (1 + s // NT))
                            load_qk(2 * k + 2 + s // NT, s // NT)
                        if s in (NT, STEPS - 1):
                            sp.wait_ge(pv_done, BLOCKS * k + BLOCKS // 2 * (1 + (s > NT)))
                            load_v(2 * k + 2 + (s > NT), int(s > NT))

                with sp.Fori(0, LOOPS - 1) as k:
                    body(k, False)
                body(LOOPS - 1, True)
                for i in range(2):
                    sp.wait_ge(stored[i], 16 * STEPS * LOOPS // 2 + 1)

            @block.tensor
            def _(pe):
                def scores(k, row, part):
                    s, h = row // R, row % R
                    gp, n = s // NT % 2, key_blocks(s)
                    if s % NT == 0 and h + part == 0:
                        pe.wait_ge(qk_in[gp], 48 * (k + s // STEPS + 1))
                    before = row_before(row, part)
                    if not (isinstance(k, int) and ROWS * k + before < 0):
                        pe.wait_ge(expd, ROWS * k + before + 1)
                    bank, banks = row_banks(row)
                    w = n * P // banks
                    lhs = q[:, gp, h, tile_of(s) * P:(tile_of(s) + 1) * P]
                    keys = slice(part * w, (part + 1) * w)
                    out = psum[:, bank + part, 0:w]
                    pe.matmul(out, lhs, kk[:, gp, 0, keys], start=True, stop=False)
                    if keys.stop == n * P:
                        pe.matmul(out[:, w - P:w], const.ident_r[:, :], const.mask[:, :], start=False, stop=False)
                    done = pe.matmul(out, lhs, kk[:, gp, 1, keys], start=False, stop=True)
                    if ends_row(row, part):
                        done.then_inc(scored, 1)

                def turn(k, b):
                    s = step_of(b)
                    j = b - first_block(s)
                    if j == 0:
                        pe.wait_ge(expd, ROWS * k + R * (s + 1))
                    if not (isinstance(k, int) and BLOCKS * k + b < 2):
                        pe.wait_ge(lo_done, BLOCKS * k + b - 1)
                    for h in range(R):
                        done = pe.transpose(psum[:, T_BANK + b % 2, h * P:(h + 1) * P],
                                            row_probs(s, h)[:, j * P:(j + 1) * P], const.ident[:, :])
                    done.then_inc(turned, 1)

                def times_v(k, b):
                    s = step_of(b)
                    j, gp = b - first_block(s), s // NT % 2
                    if j == 0:
                        if s % NT == 0:
                            pe.wait_ge(v_in[gp], 16 * (k + s // STEPS + 1))
                        if not (isinstance(k, int) and STEPS * k + s < 2):
                            pe.wait_ge(scaled, STEPS * k + s - 1 + 2)
                    pe.wait_ge(lo_done, BLOCKS * k + b + 1)
                    for z in range(2):
                        done = pe.matmul(psum[:, O_BANK + s % 2, :], v[:, gp, j, :], pt[:, b % PTR, z, :],
                                         start=j == 0 and z == 0, stop=j == key_blocks(s) - 1 and z == 1)
                    done.then_inc(pv_done, 1)

                def turn_out(k, s):
                    pe.wait_ge(o_copied, STEPS * k + s + 1)
                    for h in range(R):
                        done = pe.matmul(psum[:, O_BANK + s % 2, h * HD:(h + 1) * HD], o_t[:, s % 2, h * P:(h + 1) * P],
                                         const.fold[:, :], start=True, stop=True)
                    done.then_inc(o_turned, 1)

                def run(k, part):
                    for i, parts, block_t, block_v, _, out in positions(part):
                        for s in out:
                            turn_out(k, s)
                        if block_t is not None:
                            turn(k, block_t)
                        for row, bank in parts:
                            scores(k, row, bank)
                        if block_v is not None:
                            times_v(k, block_v)

                run(0, "prologue")
                with pe.Fori(0, LOOPS - 1) as k:
                    run(k, "body")
                run(LOOPS - 1, "last")

            @block.scalar
            def _(act):
                def exp(k, row):
                    s, h = row // R, row % R
                    n = key_blocks(s)
                    bank, banks = row_banks(row)
                    act.wait_ge(topped, ROWS * k + row + 1)
                    at = row % ROWS
                    act.activation(row_probs(s, h).rearrange("p (a w) -> p a w", a=banks),
                                   row_view(psum[:, bank:bank + banks, :], n), ACT.Exp, bias=top[:, at:at + 1],
                                   accum_out=sums[:, at:at + 1]).then_inc(expd, 1)

                def run(k, part):
                    for i, _, b, _, copy, _ in positions(part):
                        for s in copy:
                            act.wait_ge(pv_done, BLOCKS * k + first_block(s + 1))
                            act.activation(o_t[:, s % 2, :], psum[:, O_BANK + s % 2, :], ACT.Copy).then_inc(o_copied, 1)
                        if b is not None:
                            act.wait_ge(turned, BLOCKS * k + b + 1)
                            act.activation(pt[:, b % PTR, 0, :], psum[:, T_BANK + b % 2, :], ACT.Copy).then_inc(hi_done, 1)
                        for row in exps_at(i - 1)[1] + exps_at(i)[0]:
                            if part != "last" or row < ROWS:
                                exp(k, row)

                run(0, "prologue")
                with act.Fori(0, LOOPS - 1) as k:
                    run(k, "body")
                run(LOOPS - 1, "last")

            @block.vector
            def _(dve):
                dve.sem_inc(scaled, 2)
                for i in range(2):
                    dve.sem_inc(stored[i], 1)

                def maximum(k, row):
                    bank, banks = row_banks(row)
                    at = row % ROWS
                    dve.wait_ge(scored, ROWS * k + row + 1)
                    dve.tensor_reduce(top[:, at:at + 1], row_view(psum[:, bank:bank + banks, :], key_blocks(row // R)),
                                      AX.XY, ALU.max, negate=True).then_inc(topped, 1)

                def run(k, part):
                    for i, parts, b, _, copy, out in positions(part):
                        for s in out:
                            at = s % 2
                            dve.wait_ge(inverted, STEPS * k + s + 1)
                            dve.wait_ge(stored[at], 16 * (STEPS // 2 * k + s // 2) + 1)
                            dve.wait_ge(o_turned, STEPS * k + s + 1)
                            dve.tensor_tensor(res[:, at], psum[:, O_BANK + at, 0:R * HD].rearrange("p (h d) -> p h d", d=HD),
                                              inv[:, at, :, None].broadcast_to([P, R, HD]), ALU.mult).then_inc(scaled, 1)
                        for row in [r for r, p in parts if ends_row(r, p)]:
                            maximum(k, row)
                        if b is not None:
                            dve.wait_ge(hi_done, BLOCKS * k + b + 1)
                            dve.tensor_tensor(pt[:, b % PTR, 1, :], psum[:, T_BANK + b % 2, :],
                                              raw(pt[:, b % PTR, 0, :]), ALU.subtract).then_inc(lo_done, 1)
                        for s in copy:
                            dve.wait_ge(scaled, STEPS * k + s + 1)
                            dve.wait_ge(expd, ROWS * k + R * (s + 1))
                            dve.reciprocal(inv[:, s % 2, :], sums[:, s % STEPS * R:(s % STEPS + 1) * R]
                                           ).then_inc(inverted, 1)

                run(0, "prologue")
                with dve.Fori(0, LOOPS - 1) as k:
                    run(k, "body")
                run(LOOPS - 1, "last")


def stage_c(nc, dims, dram, const, psum):
    D, G, S, B, E = dims.D, dims.G, dims.S, dims.B, dims.E
    KC = D // P
    TPC = 2
    CH = TPC * P
    NCH = B * S // CH
    LOOPS = NCH // 2
    CPB = S // CH
    NT = 2 * TPC
    XR = 2 * TPC + 2
    UP_BANKS = 2
    WX = D + E
    EB = 3
    EN = WX // EB
    GATE_BANK, GATE_COL = EB - 1, D - (EB - 1) * EN
    assert WX % EB == 0 and EN <= 512 and EN % 2 == 0
    with ExitStack() as c:
        def sb(name, shape, dt=F32):
            return c.enter_context(nc.sbuf_tensor(name, shape, dt))

        def sem(name):
            return c.enter_context(nc.semaphore(name))

        wup = sb("wup_t", [P, 2, KC, D], F32R)
        wex = sb("wex", [P, 2, KC, WX], F32R)
        yt = sb("yt", [P, 2, 2, KC, CH], F32R)
        y = sb("y", [P, 2 * TPC, D])
        att = sb("att_sb", [P, 2, D])
        h_out = sb("h_out", [P, 4, CH])
        w_raw = y
        stats = sb("stats", [P, 2, 2, 6])
        mv = sb("mv", [P, 2 * TPC, 2])
        std = sb("std", [P, 2 * TPC])
        rstd = sb("rstd", [P, 2 * TPC])
        eps = sb("eps_c", [P, 1])
        best = sb("best", [P, 2 * TPC, 8])
        nbest = sb("nbest", [P, 2 * TPC])
        ex = sb("ex", [P, 2 * TPC, 2])
        ex_sum = sb("ex_sum", [P, 2 * TPC])
        ex_inv = sb("ex_inv", [P, 2 * TPC])
        route = sb("route", [P, 2 * TPC, 2])
        route_sum = sb("route_sum", [P, 2 * TPC])
        idle = sem("c_idle")
        w_in = [sem(f"c_w_in{i}") for i in range(4)]
        w_zero = sem("c_w_zero")
        w_turned, w_hi, w_lo = sem("c_w_turned"), sem("c_w_hi"), sem("c_w_lo")
        x_in = [sem(f"c_x_in{i}") for i in range(2 * TPC)]
        att_in = [sem(f"c_att_in{i}") for i in range(2)]
        chain = sem("c_chain")
        var_done, std_done = sem("c_var_done"), sem("c_std_done")
        y_done = sem("c_y_done")
        turned, t_hi, t_lo = sem("c_turned"), sem("c_t_hi"), sem("c_t_lo")
        up_done = sem("c_up_done")
        relu_done = sem("c_relu_done")
        h_stored = [sem(f"c_h_stored{i}") for i in range(4)]
        exp_done_pe = sem("c_expert_done")
        e_free = sem("c_e_free")
        nbest_done, soft_done = sem("c_nbest_done"), sem("c_soft_done")
        r_done = sem("c_r_done")
        r_stored = [sem(f"c_r_stored{i}") for i in range(2 * TPC)]

        EB_ORDER = [GATE_BANK] + [b for b in range(EB) if b != GATE_BANK]
        E_BANK0 = 2 + UP_BANKS

        w_tiles = 2 * KC + 1
        turn_groups = 2 * KC + 2

        with nc.Block() as block:

            @block.sync
            def _(sp):
                for i in range(w_tiles):
                    if i >= 4:
                        j = i - 4
                        if j < KC + 1:
                            sp.wait_ge(w_turned, 2 * (j + 1))
                        else:
                            sp.wait_ge(w_lo, turn_groups + j - KC)
                    dst = w_raw[:, i % 4, :]
                    if i < KC:
                        sp.dma_start(dst, dram.wup[i * P:(i + 1) * P, :]).then_inc(w_in[i % 4], 16)
                    elif i == KC:
                        sp.wait_ge(w_zero, 1)
                        sp.dma_start(dst[0:E, :], dram.wg[:, :]).then_inc(w_in[i % 4], 16)
                    else:
                        e = i - KC - 1
                        sp.dma_start(dst, dram.wex[e * P:(e + 1) * P, :]).then_inc(w_in[i % 4], 16)
                sp.wait_ge(w_lo, turn_groups + KC)

                def load(k, t):
                    tile = 2 * TPC * k + t
                    sp.dma_start(y[:, t, :], dram.x[bass.ds(tile, 1)].rearrange("a p n -> (a p) n")
                                 ).then_inc(x_in[t], 16)
                    sp.dma_start(att[:, t % 2, :], dram.att_tiles[bass.ds(tile, 1)].rearrange("a p n -> (a p) n")
                                 ).then_inc(att_in[t % 2], 16)

                for t in range(2 * TPC):
                    if t >= 2:
                        sp.wait_ge(y_done, t - 1)
                    load(0, t)

                def chunk(k, par, loads):
                    ch = 2 * k + par
                    for n in range(KC):
                        sp.wait_ge(relu_done, KC * ch + n + 1 + UP_BANKS)
                        sp.dma_start(dram.h[bass.ds(TPC * ch, TPC), :, n, :].rearrange("a p t -> p a t"),
                                     h_out[:, n % 4, :].rearrange("p (a t) -> p a t", a=TPC)).then_inc(h_stored[n % 4], 16)
                    for i in range(TPC):
                        t = TPC * par + i
                        sp.wait_ge(e_free, EB * (TPC * ch + i + 1) + EB)
                        sp.dma_start(dram.r[bass.ds(2 * TPC * k + t, 1)].rearrange("a p n -> (a p) n"), y[:, t, :]
                                     ).then_inc(r_stored[t], 16)
                    for i in range(TPC if loads else 0):
                        t = TPC * par + i
                        sp.wait_ge(r_stored[t], 16 * (k + 1))
                        sp.wait_ge(y_done, TPC * (ch + 2))
                        load(k + 1, t)

                with sp.Fori(0, LOOPS - 1) as k:
                    chunk(k, 0, True)
                    chunk(k, 1, True)
                chunk(LOOPS - 1, 0, False)
                chunk(LOOPS - 1, 1, False)
                for i in range(4):
                    sp.wait_ge(h_stored[i], 16 * KC * NCH // 4 + 1)
                for t in range(2 * TPC):
                    sp.wait_ge(r_stored[t], 16 * LOOPS)

            @block.gpsimd
            def _(pool):
                pool.wait_ge(w_turned, 2 * (KC - 4 + 1))
                pool.memset(w_raw[:, KC % 4, :], 0.0).then_inc(w_zero, 1)

            @block.tensor
            def _(pe):
                for n in range(turn_groups):
                    i, half = n // 2, n % 2
                    if half == 0:
                        pe.wait_ge(w_in[i % 4], 16 * (i // 4 + 1))
                    if n >= 2:
                        pe.wait_ge(w_lo, n - 1)
                    for a in range(4):
                        e = 4 * half + a
                        done = pe.transpose(psum[:, n % 2, a * P:(a + 1) * P], w_raw[:, i % 4, e * P:(e + 1) * P],
                                            const.ident[:, :])
                    done.then_inc(w_turned, 1)

                def turn(ch, par, n):
                    i, half = n // 2, n % 2
                    pe.wait_ge(y_done, TPC * ch + i + 1)
                    if isinstance(ch, int) and NT * ch + n < 2:
                        pe.wait_ge(w_lo, turn_groups)
                    else:
                        pe.wait_ge(t_lo, NT * ch + n - 1)
                    for a in range(4):
                        e = 4 * half + a
                        done = pe.transpose(psum[:, n % 2, a * P:(a + 1) * P], y[:, TPC * par + i, e * P:(e + 1) * P],
                                            const.ident[:, :])
                    done.then_inc(turned, 1)

                for n in range(NT):
                    turn(0, 0, n)
                pe.wait_ge(w_lo, turn_groups + KC)
                pe.wait_ge(w_hi, turn_groups + KC)

                def chunk(k, par, more):
                    ch = 2 * k + par
                    pe.wait_ge(t_lo, NT * (ch + 1))
                    for n in range(KC):
                        pe.wait_ge(relu_done, KC * ch + n + 1)
                        for e in range(KC):
                            for zw, zx in ((0, 0), (0, 1), (1, 0)):
                                done = pe.matmul(psum[:, 2 + n % UP_BANKS, 0:CH], wup[:, zw, e, n * P:(n + 1) * P],
                                                 yt[:, par, zx, e, :], start=e == 0 and zw + zx == 0,
                                                 stop=e == KC - 1 and zw == 1)
                        done.then_inc(up_done, 1)
                    for m in range(TPC * EB):
                        i, b = m // EB, EB_ORDER[m % EB]
                        pe.wait_ge(e_free, TPC * EB * ch + m + 1)
                        for e in range(KC):
                            for zw, zx in ((0, 0), (0, 1), (1, 0)):
                                done = pe.matmul(psum[:, E_BANK0 + b, 0:EN], yt[:, par, zx, e, i * P:(i + 1) * P],
                                                 wex[:, zw, e, b * EN:(b + 1) * EN], start=e == 0 and zw + zx == 0,
                                                 stop=e == KC - 1 and zw == 1)
                        done.then_inc(exp_done_pe, 1)
                        if more and 1 <= m <= NT:
                            turn(ch + 1, 1 - par, m - 1)

                with pe.Fori(0, LOOPS - 1) as k:
                    chunk(k, 0, True)
                    chunk(k, 1, True)
                chunk(LOOPS - 1, 0, True)
                chunk(LOOPS - 1, 1, False)

            @block.scalar
            def _(act):
                for n in range(turn_groups):
                    i, half = n // 2, n % 2
                    act.wait_ge(w_turned, n + 1)
                    src = psum[:, n % 2, :].rearrange("p (a t) -> p a t", a=4)
                    dst = wup[:, 0, 4 * half:4 * half + 4, i * P:(i + 1) * P] if i < KC else \
                        wex[:, 0, 4 * half:4 * half + 4, D:WX]
                    act.activation(dst, src if i < KC else src[:, :, 0:E], ACT.Copy).then_inc(w_hi, 1)
                for e in range(KC):
                    i = KC + 1 + e
                    act.wait_ge(w_in[i % 4], 16 * (i // 4 + 1))
                    act.activation(wex[:, 0, e, 0:D], w_raw[:, i % 4, :], ACT.Copy).then_inc(w_hi, 1)

                def root(ch, par):
                    act.wait_ge(var_done, TPC * (ch + 1))
                    act.activation(std[:, TPC * par:TPC * par + TPC], mv[:, TPC * par:TPC * par + TPC, 1], ACT.Sqrt,
                                   bias=eps[:, 0:1]).then_inc(std_done, 1)

                def t_high(ch, par, n):
                    i, half = n // 2, n % 2
                    act.wait_ge(turned, NT * ch + n + 1)
                    act.activation(yt[:, par, 0, 4 * half:4 * half + 4, i * P:(i + 1) * P],
                                   psum[:, n % 2, :].rearrange("p (a t) -> p a t", a=4), ACT.Copy).then_inc(t_hi, 1)

                root(0, 0)
                for n in range(NT):
                    t_high(0, 0, n)

                def chunk(k, par, more):
                    ch = 2 * k + par
                    for n in range(KC):
                        act.wait_ge(up_done, KC * ch + n + 1)
                        act.wait_ge(h_stored[n % 4], 16 * (KC // 4 * ch + n // 4) + 1)
                        act.activation(h_out[:, n % 4, :], psum[:, 2 + n % UP_BANKS, 0:CH], ACT.Relu
                                       ).then_inc(relu_done, 1)
                        if n == 5 and more:
                            root(ch + 1, 1 - par)
                    for m in range(TPC * EB):
                        i, t = m // EB, TPC * par + m // EB
                        if m % EB == 0:
                            act.wait_ge(nbest_done, TPC * ch + i + 1)
                            act.activation(ex[:, t, :], best[:, t, 0:2], ACT.Exp, bias=nbest[:, t:t + 1],
                                           accum_out=ex_sum[:, t:t + 1]).then_inc(soft_done, 1)
                        if more and 1 <= m <= NT:
                            t_high(ch + 1, 1 - par, m - 1)

                with act.Fori(0, LOOPS - 1) as k:
                    chunk(k, 0, True)
                    chunk(k, 1, True)
                chunk(LOOPS - 1, 0, True)
                chunk(LOOPS - 1, 1, False)

            @block.vector
            def _(dve):
                dve.memset(eps[:, :], EPS).then_inc(chain, 1)
                dve.sem_inc(relu_done, UP_BANKS)
                dve.sem_inc(e_free, EB)
                for i in range(4):
                    dve.sem_inc(h_stored[i], 1)
                for n in range(turn_groups):
                    i, half = n // 2, n % 2
                    dve.wait_ge(w_hi, n + 1)
                    src = psum[:, n % 2, :].rearrange("p (a t) -> p a t", a=4)
                    dst = wup[:, :, 4 * half:4 * half + 4, i * P:(i + 1) * P] if i < KC else \
                        wex[:, :, 4 * half:4 * half + 4, D:WX]
                    dve.tensor_tensor(dst[:, 1], src if i < KC else src[:, :, 0:E], raw(dst[:, 0]), ALU.subtract
                                      ).then_inc(w_lo, 1)
                for e in range(KC):
                    dve.wait_ge(w_hi, turn_groups + e + 1)
                    dve.tensor_tensor(wex[:, 1, e, 0:D], w_raw[:, (KC + 1 + e) % 4, :], raw(wex[:, 0, e, 0:D]),
                                      ALU.subtract).then_inc(w_lo, 1)
                LINKS = 7
                STEP = LINKS + 3 * TPC

                def norm(k, ch, par, base):
                    for i in range(TPC):
                        t = TPC * par + i
                        dve.wait_ge(x_in[t], 16 * (k + 1))
                        dve.wait_ge(att_in[t % 2], 16 * (2 * k + t // 2 + 1))
                        dve.tensor_tensor(y[:, t, :], y[:, t, :], att[:, t % 2, :], ALU.add).then_inc(chain, 1)
                    for i in range(TPC):
                        t = TPC * par + i
                        dve.wait_ge(chain, base + i + 1)
                        for half in range(2):
                            dve.bn_stats(stats[:, i, half, :], y[:, t, half * 512:(half + 1) * 512]).then_inc(chain, 1)
                    dve.wait_ge(chain, base + TPC + 2 * TPC)
                    dve.sem_inc(idle, 1)
                    for i in range(TPC):
                        t = TPC * par + i
                        dve.bn_aggr(mv[:, t, :], stats[:, i].rearrange("p a b -> p (a b)")).then_inc(var_done, 1)
                    dve.wait_ge(std_done, ch + 1)
                    dve.reciprocal(rstd[:, TPC * par:TPC * par + TPC], std[:, TPC * par:TPC * par + TPC]
                                   ).then_inc(chain, 1)
                    dve.wait_ge(chain, base + LINKS)
                    for i in range(TPC):
                        t = TPC * par + i
                        dve.tensor_scalar(y[:, t, :], y[:, t, :], mv[:, t, 0:1], rstd[:, t:t + 1], ALU.subtract,
                                          ALU.mult).then_inc(y_done, 1)

                def t_low(ch, par, n):
                    i, half = n // 2, n % 2
                    dve.wait_ge(t_hi, NT * ch + n + 1)
                    at = yt[:, par, :, 4 * half:4 * half + 4, i * P:(i + 1) * P]
                    dve.tensor_tensor(at[:, 1], psum[:, n % 2, :].rearrange("p (a t) -> p a t", a=4), raw(at[:, 0]),
                                      ALU.subtract).then_inc(t_lo, 1)

                norm(0, 0, 0, 1)
                for n in range(NT):
                    t_low(0, 0, n)

                def chunk(k, par, more):
                    ch = 2 * k + par
                    base = 1 + LINKS + STEP * ch
                    if more:
                        norm(k + par, ch + 1, 1 - par, base)
                    base = base + (LINKS if more else 0)
                    for m in range(TPC * EB):
                        i, t, b = m // EB, TPC * par + m // EB, EB_ORDER[m % EB]
                        dve.wait_ge(exp_done_pe, TPC * EB * ch + m + 1)
                        if m % EB == 0:
                            dve.sem_inc(idle, 1)
                            dve.max(best[:, t, :], psum[:, E_BANK0 + b, GATE_COL:GATE_COL + E]).then_inc(chain, 1)
                            dve.wait_ge(chain, base + 3 * i + 1)
                            dve.tensor_scalar(nbest[:, t:t + 1], best[:, t, 0:1], -1.0, None, ALU.mult
                                              ).then_inc(nbest_done, 1)
                            dve.wait_ge(soft_done, TPC * ch + i + 1)
                            dve.reciprocal(ex_inv[:, t:t + 1], ex_sum[:, t:t + 1]).then_inc(chain, 1)
                            dve.wait_ge(chain, base + 3 * i + 2)
                            dve.tensor_scalar(route[:, t, :], ex[:, t, :], ex_inv[:, t:t + 1], 0.0, ALU.mult, ALU.add,
                                              accum_out=route_sum[:, t:t + 1]).then_inc(chain, 1)
                            dve.wait_ge(chain, base + 3 * i + 3)
                        w = EN if b < EB - 1 else GATE_COL
                        cols = slice(b * EN, b * EN + w)
                        dve.scalar_tensor_tensor(y[:, t, cols], psum[:, E_BANK0 + b, 0:w], route_sum[:, t:t + 1],
                                                 y[:, t, cols], op0=ALU.mult, op1=ALU.add).then_inc(e_free, 1)
                        if more and 1 <= m <= NT:
                            t_low(ch + 1, 1 - par, m - 1)

                with dve.Fori(0, LOOPS - 1) as k:
                    chunk(k, 0, True)
                    chunk(k, 1, True)
                chunk(LOOPS - 1, 0, True)
                chunk(LOOPS - 1, 1, False)


def stage_d(nc, dims, dram, const, psum):
    D, S, B = dims.D, dims.S, dims.B
    KC = D // P
    NTILES = B * S // P
    TB = 4
    LOOPS = NTILES // TB
    HALVES, HW = 2, D // 2
    turn_groups = 2 * KC
    with ExitStack() as c:
        def sb(name, shape, dt=F32):
            return c.enter_context(nc.sbuf_tensor(name, shape, dt))

        def sem(name):
            return c.enter_context(nc.semaphore(name))

        wd = sb("wdown_t", [P, 2, KC, D], F32R)
        w_raw = sb("w_raw_d", [P, 4, D])
        h_raw = sb("h_raw", [P, 2, KC, P])
        ht = sb("ht", [P, 2, 2, KC, P], F32R)
        r = sb("r_sb", [P, TB, D])
        stats = sb("stats_d", [P, 2, HALVES, 6])
        mv = sb("mv_d", [P, 2, 2])
        std = sb("std_d", [P, 2])
        rstd = sb("rstd_d", [P, 2])
        eps = sb("eps_d", [P, 1])
        idle = sem("d_idle")
        w_in = [sem(f"d_w_in{i}") for i in range(4)]
        w_turned, w_hi, w_lo = sem("d_w_turned"), sem("d_w_hi"), sem("d_w_lo")
        h_in = [sem(f"d_h_in{i}") for i in range(2)]
        r_in = [sem(f"d_r_in{i}") for i in range(TB)]
        h_hi, h_lo = sem("d_h_hi"), sem("d_h_lo")
        done_half = sem("d_done_half")
        added = sem("d_added")
        counted, var_done, std_done, inverted = sem("d_counted"), sem("d_var_done"), sem("d_std_done"), sem("d_inverted")
        normed = sem("d_normed")
        eps_set = sem("d_eps_set")
        stored = [sem(f"d_stored{i}") for i in range(TB)]
        BANK0 = 2

        with nc.Block() as block:

            @block.sync
            def _(sp):
                def load_h(tile, par):
                    sp.dma_start(h_raw[:, par], dram.h[bass.ds(tile, 1)].rearrange("a p n t -> (a p) n t")
                                 ).then_inc(h_in[par], 16)

                def load_r(tile, t):
                    sp.dma_start(r[:, t, :], dram.r[bass.ds(tile, 1)].rearrange("a p n -> (a p) n")
                                 ).then_inc(r_in[t], 16)

                for i in range(KC):
                    if i >= 4:
                        sp.wait_ge(w_turned, 2 * (i - 3))
                    sp.dma_start(w_raw[:, i % 4, :], dram.wdown[i * P:(i + 1) * P, :]).then_inc(w_in[i % 4], 16)
                for t in range(2):
                    load_h(t, t)
                for t in range(TB - 1):
                    load_r(t, t)
                sp.wait_ge(h_lo, 1)
                load_h(2, 0)

                def step(k, t, more_h, more_r, first):
                    if more_h:
                        sp.wait_ge(h_lo, TB * k + t + 2)
                        load_h(TB * k + t + 3, (t + 1) % 2)
                    sp.wait_ge(normed, TB * k + t + 1)
                    sp.dma_start(dram.out[bass.ds(TB * k + t, 1)].rearrange("a p n -> (a p) n"), r[:, t, :]
                                 ).then_inc(stored[t], 16)
                    if more_r:
                        if t >= 1:
                            sp.wait_ge(stored[t - 1], 16 * (k + 1))
                        elif not first:
                            sp.wait_ge(stored[TB - 1], 16 * k)
                        load_r(TB * k + t + TB - 1, (t + TB - 1) % TB)

                for t in range(TB):
                    step(0, t, True, True, True)
                with sp.Fori(1, LOOPS - 1) as k:
                    for t in range(TB):
                        step(k, t, True, True, False)
                for t in range(TB):
                    step(LOOPS - 1, t, t + 3 < TB, t + TB - 1 < TB, False)
                for t in range(TB):
                    sp.wait_ge(stored[t], 16 * LOOPS)

            @block.tensor
            def _(pe):
                for n in range(turn_groups):
                    i, half = n // 2, n % 2
                    if half == 0:
                        pe.wait_ge(w_in[i % 4], 16 * (i // 4 + 1))
                    if n >= 2:
                        pe.wait_ge(w_lo, n - 1)
                    for a in range(4):
                        e = 4 * half + a
                        done = pe.transpose(psum[:, n % 2, a * P:(a + 1) * P], w_raw[:, i % 4, e * P:(e + 1) * P],
                                            const.ident[:, :])
                    done.then_inc(w_turned, 1)
                pe.wait_ge(w_lo, turn_groups)
                with pe.Fori(0, LOOPS) as k:
                    for t in range(TB):
                        par = t % 2
                        pe.wait_ge(h_lo, TB * k + t + 1)
                        for half in range(HALVES):
                            bank = BANK0 + HALVES * par + half
                            pe.wait_ge(added, HALVES * (TB * k + t) + half + 1)
                            for e in range(KC):
                                for zh, zw in ((0, 0), (0, 1), (1, 0)):
                                    done = pe.matmul(psum[:, bank, :], ht[:, par, zh, e, :],
                                                     wd[:, zw, e, half * HW:(half + 1) * HW],
                                                     start=e == 0 and zh + zw == 0, stop=e == KC - 1 and zh == 1)
                            done.then_inc(done_half, 1)

            @block.scalar
            def _(act):
                for n in range(turn_groups):
                    i, half = n // 2, n % 2
                    act.wait_ge(w_turned, n + 1)
                    act.activation(wd[:, 0, 4 * half:4 * half + 4, i * P:(i + 1) * P],
                                   psum[:, n % 2, :].rearrange("p (a t) -> p a t", a=4), ACT.Copy).then_inc(w_hi, 1)

                def high(k, t):
                    act.wait_ge(h_in[t % 2], 16 * (TB // 2 * k + t // 2 + 1))
                    if not (isinstance(k, int) and TB * k + t < 2):
                        act.wait_ge(done_half, HALVES * (TB * k + t - 1))
                    act.activation(ht[:, t % 2, 0], h_raw[:, t % 2], ACT.Copy).then_inc(h_hi, 1)

                def step(k, t, more):
                    if more:
                        high(k + (t + 1) // TB, (t + 1) % TB)
                    act.wait_ge(var_done, TB * k + t + 1)
                    act.activation(std[:, t % 2:t % 2 + 1], mv[:, t % 2, 1:2], ACT.Sqrt, bias=eps[:, 0:1]
                                   ).then_inc(std_done, 1)

                act.wait_ge(eps_set, 1)
                high(0, 0)
                for t in range(TB):
                    step(0, t, True)
                with act.Fori(1, LOOPS - 1) as k:
                    for t in range(TB):
                        step(k, t, True)
                for t in range(TB):
                    step(LOOPS - 1, t, t + 1 < TB)

            @block.vector
            def _(dve):
                dve.memset(eps[:, :], EPS).then_inc(eps_set, 1)
                dve.sem_inc(added, 2 * HALVES)
                for n in range(turn_groups):
                    i, half = n // 2, n % 2
                    dve.wait_ge(w_hi, n + 1)
                    at = wd[:, :, 4 * half:4 * half + 4, i * P:(i + 1) * P]
                    dve.tensor_tensor(at[:, 1], psum[:, n % 2, :].rearrange("p (a t) -> p a t", a=4), raw(at[:, 0]),
                                      ALU.subtract).then_inc(w_lo, 1)

                def low(k, t):
                    dve.wait_ge(h_hi, TB * k + t + 1)
                    dve.tensor_tensor(ht[:, t % 2, 1], h_raw[:, t % 2], raw(ht[:, t % 2, 0]), ALU.subtract
                                      ).then_inc(h_lo, 1)

                def step(k, t, more):
                    if more:
                        low(k + (t + 1) // TB, (t + 1) % TB)
                    par, tile = t % 2, TB * k + t
                    dve.wait_ge(r_in[t], 16 * (k + 1))
                    for half in range(HALVES):
                        cols = slice(half * HW, (half + 1) * HW)
                        dve.wait_ge(done_half, HALVES * tile + half + 1)
                        dve.tensor_tensor(r[:, t, cols], psum[:, BANK0 + HALVES * par + half, :], r[:, t, cols], ALU.add
                                          ).then_inc(added, 1)
                        dve.wait_ge(added, HALVES * tile + half + 1 + 2 * HALVES)
                        dve.bn_stats(stats[:, par, half, :], r[:, t, cols]).then_inc(counted, 1)
                    dve.wait_ge(counted, HALVES * (tile + 1))
                    dve.sem_inc(idle, 1)
                    dve.bn_aggr(mv[:, par, :], stats[:, par].rearrange("p a b -> p (a b)")).then_inc(var_done, 1)
                    dve.wait_ge(std_done, tile + 1)
                    dve.reciprocal(rstd[:, par:par + 1], std[:, par:par + 1]).then_inc(inverted, 1)
                    dve.wait_ge(inverted, tile + 1)
                    dve.tensor_scalar(r[:, t, :], r[:, t, :], mv[:, par, 0:1], rstd[:, par:par + 1], ALU.subtract,
                                      ALU.mult).then_inc(normed, 1)

                low(0, 0)
                with dve.Fori(0, LOOPS - 1) as k:
                    for t in range(TB):
                        step(k, t, True)
                for t in range(TB):
                    step(LOOPS - 1, t, t + 1 < TB)


def post_ln_layer(nc, x, wq, bq, wk, bk, wv, bv, wup, wdown, wg, wex, out):
    dims, dram, const = Names(), Names(), Names()
    dims.B, dims.S, dims.D = x.shape
    dims.H, _, dims.HD = wq.shape
    dims.G = wk.shape[0]
    dims.E = wg.shape[0]
    B, S, D, H, G, HD = dims.B, dims.S, dims.D, dims.H, dims.G, dims.HD

    def scratch(name, *shape):
        return nc.dram_tensor(name, shape, F32, kind="Internal").ap()

    dram.x = x.rearrange("b (i p) n -> (b i) p n", p=P)
    dram.out = out.rearrange("b (i p) n -> (b i) p n", p=P)
    dram.wq, dram.wk, dram.wv = wq, wk, wv
    dram.bq = bq.rearrange("h (d a) -> (h d) a", a=1)
    dram.bk = bk.rearrange("g (d a) -> (g d) a", a=1)
    dram.bv = bv.rearrange("(a g) d -> a (g d)", a=1)
    dram.wup, dram.wdown, dram.wg, dram.wex = wup, wdown, wg, wex
    dram.q = scratch("q_split", B * G, H // G, 2 * HD, S)
    dram.k = scratch("k_split", B * G, 2, HD, S)
    dram.v = scratch("v_split", B * G, S, 2 * HD)
    dram.att = scratch("attention", B, S, G, H // G * HD)
    dram.att_tiles = dram.att.rearrange("b (i p) g n -> (b i) p (g n)", p=P)
    dram.h = scratch("hidden_t", B * S // P, P, D // P, P)
    dram.r = scratch("residual", B * S // P, P, D)

    with ExitStack() as c:
        psum_t = c.enter_context(nc.psum_tensor("banks", [P, 8, 512], F32))
        const.ident = c.enter_context(nc.sbuf_tensor("ident", [P, P], F32))
        const.ident_r = c.enter_context(nc.sbuf_tensor("ident_r", [P, P], F32R))
        const.mask = c.enter_context(nc.sbuf_tensor("mask", [P, P], F32R))
        const.fold = c.enter_context(nc.sbuf_tensor("fold", [P, HD], F32))
        constants(nc, const)
        stage_a(nc, dims, dram, const, psum_t)
        stage_b(nc, dims, dram, const, psum_t)
        stage_c(nc, dims, dram, const, psum_t)
        stage_d(nc, dims, dram, const, psum_t)


_INS = ["L0_attn_x", "L0_attn_Wq", "L0_attn_bq", "L0_attn_Wk", "L0_attn_bk", "L0_attn_Wv", "L0_attn_bv",
        "L0_ffn_W_up", "L0_ffn_W_down", "L0_ffn_W_gate", "L0_ffn_W_expert"]


def kernel(**inputs):
    import numpy as _np
    import concourse.bacc as _bacc
    from concourse import mybir as _mybir
    from concourse.bass_utils import run_bass_kernel_spmd as _run

    nc = _bacc.Bacc("TRN2", target_bir_lowering=False, num_devices=1)
    arrays, args = {}, []
    for name in _INS:
        a = _np.ascontiguousarray(inputs[name])
        arrays[f"in_{name}"] = a
        args.append(nc.dram_tensor(f"in_{name}", a.shape, _mybir.dt.from_np(a.dtype), kind="ExternalInput").ap())
    shape = arrays["in_L0_attn_x"].shape
    args.append(nc.dram_tensor("out_dram", shape, _mybir.dt.float32, kind="ExternalOutput").ap())
    post_ln_layer(nc, *args)
    r = _run(nc, [arrays], core_ids=[0])
    return r.results[0]["out_dram"]
```

```python
from contextlib import ExitStack

import numpy as np

import concourse.bass as bass
from concourse import mybir
from concourse.alu_op_type import AluOpType as ALU

F32 = mybir.dt.float32
F32R = mybir.dt.float32r
BF16 = mybir.dt.bfloat16
ACT = mybir.ActivationFunctionType
AX = mybir.AxisListType
P = 128
EPS = 1e-5
MASKED = -3.0e38


class Names:
    pass


def raw(ap):
    return ap.bitcast(F32)


def wdown_raw(const, i):
    return const.w_raw[:, i, :] if i < 4 else const.att[:, i - 4, :]


def constants(nc, const):
    with ExitStack() as c:
        mask_f = c.enter_context(nc.sbuf_tensor("mask_f", [P, P], F32))
        made = c.enter_context(nc.semaphore("constants_made"))
        rounded = c.enter_context(nc.semaphore("constants_rounded"))
        with nc.Block() as block:

            @block.gpsimd
            def _(pool):
                pool.memset(const.ident[:, :], 0.0).then_inc(made, 1)
                pool.memset(mask_f[:, :], 0.0).then_inc(made, 1)
                pool.wait_ge(made, 2)
                pool.affine_select(out=const.ident[:, :], in_=const.ident[:, :], compare_op=ALU.not_equal, fill=1.0,
                                   base=0, pattern=[[-1, P]], channel_multiplier=1).then_inc(made, 1)
                pool.affine_select(out=mask_f[:, :], in_=mask_f[:, :], compare_op=ALU.is_ge, fill=MASKED, base=0,
                                   pattern=[[-1, P]], channel_multiplier=1).then_inc(made, 1)

            @block.vector
            def _(dve):
                dve.wait_ge(made, 4)
                dve.tensor_copy(const.ident_r[:, :], const.ident[:, :]).then_inc(rounded, 1)
                dve.tensor_copy(const.mask[:, :], mask_f[:, :]).then_inc(rounded, 1)
                half = const.fold.shape[1]
                dve.tensor_tensor(const.fold[:, :], const.ident[:, 0:half], const.ident[:, half:2 * half], ALU.add
                                  ).then_inc(rounded, 1)
                dve.wait_ge(rounded, 3)


def stage_a(nc, dims, dram, const, psum):
    D, H, G, HD, S, B = dims.D, dims.H, dims.G, dims.HD, dims.S, dims.B
    KC = D // P
    CH = 512
    TPC = CH // P
    NQ, NK = H * HD // P, G * HD // P
    NQK = NQ + NK
    NG = NQK + TPC
    NT = 2 * TPC
    KV = G * HD
    RING, SLOTS = 4, 4
    TURN0 = 4
    SCALE = 1.0 / float(np.sqrt(HD))
    with ExitStack() as c:
        def sb(name, shape, dt=F32):
            return c.enter_context(nc.sbuf_tensor(name, shape, dt))

        def sem(name):
            return c.enter_context(nc.semaphore(name))

        wq = sb("wq", [P, 2, KC, D], F32R)
        wk = sb("wk", [P, 2, KC, KV], F32R)
        wv = sb("wv", [P, 2, KC, KV], F32R)
        xt0 = sb("xt0", [P, 2, KC, CH], F32R)
        NKV = KC // 2
        with nc.sbuf_tensor("w_raw", [P, NKV + NQ, D], F32) as w_raw:
            pass
        xt = [xt0, sb("xt1", [P, 2, KC, CH], F32R)]
        stage = sb("stage", [P, SLOTS, 2, CH], F32R)
        x_raw = sb("x_raw", [P, TPC, D])
        v_sum = sb("v_sum", [P, 2, KV])
        v_out = sb("v_out", [P, 2, G, 2, HD], F32R)
        bias = sb("bias", [P, NQK])
        bias_s = sb("bias_s", [P, NQK])
        bias_v = sb("bias_v", [P, KV])
        x_in = [sem(f"a_x_in{i}") for i in range(TPC)]
        w_in = [sem(f"a_w_in{i}") for i in range(NKV + NQ)]
        bias_in = sem("a_bias_in")
        bias_scaled = sem("a_bias_scaled")
        w_hi, w_lo = sem("a_w_hi"), sem("a_w_lo")
        t_done, t_hi, t_lo = sem("a_t_done"), sem("a_t_hi"), sem("a_t_lo")
        group_done = sem("a_group_done")
        qk_hi = sem("a_qk_hi")
        drained = sem("a_drained")
        stored = [sem(f"a_stored{i}") for i in range(SLOTS)]
        v_hi = sem("a_v_hi")
        v_lo = sem("a_v_lo")
        v_stored = [sem(f"a_v_stored{i}") for i in range(2)]

        NCH = B * S // CH
        x_tiles = dram.x
        w_pieces = NKV + NQ

        assert w_pieces * D <= 2 * KC * CH + SLOTS * 2 * CH

        def piece(i):
            if i >= NKV:
                n = slice((i - NKV) * P, (i - NKV + 1) * P)
                return [(wq[:, 0, :, n], wq[:, 1, :, n], w_raw[:, i, :].rearrange("p (e n) -> p e n", n=P), SCALE)]
            v = w_raw[:, i, :].rearrange("p (a s n) -> p a s n", a=2, s=2)
            return [(w[:, 0, 2 * i:2 * i + 2, :], w[:, 1, 2 * i:2 * i + 2, :], v[:, a], 1.0)
                    for a, w in enumerate((wk, wv))]

        with nc.Block() as block:

            @block.sync
            def _(sp):
                def load_x(tile, slot):
                    sp.dma_start(x_raw[:, slot, :],
                                 x_tiles[bass.ds(tile, 1), :, :].rearrange("a p n -> (a p) n")
                                 ).then_inc(x_in[slot], 16)

                def load_w(i):
                    dst = w_raw[:, i, :]
                    if i >= NKV:
                        for hh in range(P // HD):
                            sp.dma_start(dst.rearrange("p (e n) -> p e n", n=P)[:, :, hh * HD:(hh + 1) * HD],
                                         dram.wq[P // HD * (i - NKV) + hh].rearrange("(e p) d -> p e d", p=P)
                                         ).then_inc(w_in[i], 16)
                        return
                    for a, w in enumerate((dram.wk, dram.wv)):
                        for s in range(2):
                            e = (2 * i + s) * P
                            sp.dma_start(dst[:, (2 * a + s) * KV:(2 * a + s + 1) * KV].rearrange("p (g d) -> p g d", d=HD),
                                         w[:, e:e + P, :].rearrange("g p d -> p g d")).then_inc(w_in[i], 16)

                for i in range(TPC):
                    load_x(i, i)
                for i in range(w_pieces):
                    load_w(i)
                for i in range(TPC):
                    sp.wait_ge(t_done, 2 * (i + 1))
                    load_x(TPC + i, i)

                def chunk(k, par, x_next):
                    ch = 2 * k + par

                    def next_x(n):
                        j = n - TURN0
                        if j % 2 == 1 and 0 <= j < NT:
                            sp.wait_ge(t_done, NT * (ch + 1) + j + 1)
                            load_x(TPC * (ch + 2) + j // 2, j // 2)

                    for n in range(NQK):
                        m = NQK * par + n
                        slot = m % SLOTS
                        sp.wait_ge(drained, 2 * NG * k + NG * par + n + 1 + RING)
                        for z in range(2):
                            if n < NQ:
                                g, hh = n // 2, 2 * (n % 2)
                                dst = dram.q[bass.ds(k * G + g, 1), hh:hh + 2, z * HD:(z + 1) * HD,
                                             par * CH:(par + 1) * CH].rearrange("a h d t -> (a h) d t")
                            else:
                                dst = dram.k[bass.ds(k * G + 2 * (n - NQ), 2), z, :, par * CH:(par + 1) * CH]
                            sp.dma_start(dst, raw(stage[:, slot, z, :])).then_inc(stored[slot], 16)
                        if x_next:
                            next_x(n)
                    for i in range(TPC):
                        m = TPC * par + i
                        sp.wait_ge(v_lo, 2 * TPC * k + m + 1 + 2)
                        dst = dram.v[bass.ds(k * G, G), (TPC * par + i) * P:(TPC * par + i + 1) * P, :]
                        sp.dma_start(dst.rearrange("g t f -> t g f"),
                                     raw(v_out[:, i % 2]).rearrange("p g z d -> p g (z d)")
                                     ).then_inc(v_stored[i % 2], 16)
                        if x_next:
                            next_x(NQK + i)

                with sp.Fori(0, NCH // 2 - 1) as k:
                    chunk(k, 0, True)
                    chunk(k, 1, True)
                k = NCH // 2 - 1
                chunk(k, 0, False)
                chunk(k, 1, False)
                for s in range(SLOTS):
                    sp.wait_ge(stored[s], 32 * NQK * NCH // SLOTS + 1)
                for s in range(2):
                    sp.wait_ge(v_stored[s], 16 * TPC * NCH // 2 + 1)

            @block.scalar
            def _(act):
                def t_high(n, par, count):
                    act.wait_ge(t_done, count + 1)
                    act.activation(xt[par][:, 0, 4 * (n % 2):4 * (n % 2) + 4, (n // 2) * P:(n // 2 + 1) * P],
                                   psum[:, n % 2, :].rearrange("p (a t) -> p a t", a=4), ACT.Copy).then_inc(t_hi, 1)

                for m in range(NQ):
                    act.dma_start(bias[:, m:m + 1], dram.bq[m * P:(m + 1) * P, :]).then_inc(bias_in, 16)
                for m in range(NK):
                    act.dma_start(bias[:, NQ + m:NQ + m + 1], dram.bk[m * P:(m + 1) * P, :]).then_inc(bias_in, 16)
                act.dma_start(bias_v[:, :], dram.bv.broadcast_to([P, KV])).then_inc(bias_in, 16)

                for n in range(NT):
                    t_high(n, 0, n)
                for n in range(w_pieces):
                    act.wait_ge(w_in[n], 64 if n < NKV else 16 * P // HD)
                    for hi, lo, src, scale in piece(n):
                        done = act.activation(hi, src, ACT.Copy, scale=scale)
                    done.then_inc(w_hi, 1)
                act.wait_ge(w_hi, w_pieces)
                act.wait_ge(w_lo, w_pieces)
                act.wait_ge(bias_scaled, 1)

                def chunk(k, par, t_next):
                    ch = 2 * k + par
                    for n in range(NG):
                        bank = 2 + (NG * par + n) % RING
                        if n < NQK:
                            m = NQK * par + n
                            act.wait_ge(group_done, 2 * NG * k + NG * par + n + 1)
                            act.wait_ge(stored[m % SLOTS], 2 * NQK // SLOTS * 32 * k + 32 * (m // SLOTS) + 1)
                            act.activation(stage[:, m % SLOTS, 0, :], psum[:, bank, :], ACT.Identity,
                                           bias=bias_s[:, n:n + 1]).then_inc(qk_hi, 1)
                        else:
                            i = n - NQK
                            m = TPC * par + i
                            act.wait_ge(drained, 2 * NG * k + NG * par + n + 1 + RING)
                            act.wait_ge(v_stored[i % 2], 16 * (TPC * k + m // 2) + 1)
                            act.activation(v_out[:, i % 2, :, 0, :],
                                           v_sum[:, i % 2, :].rearrange("p (g d) -> p g d", d=HD),
                                           ACT.Copy).then_inc(v_hi, 1)
                        if 0 <= n - TURN0 < NT and t_next:
                            t_high(n - TURN0, 1 - par, NT * ch + NT + n - TURN0)

                with act.Fori(0, NCH // 2 - 1) as k:
                    chunk(k, 0, True)
                    chunk(k, 1, True)
                chunk(NCH // 2 - 1, 0, True)
                chunk(NCH // 2 - 1, 1, False)

            @block.vector
            def _(dve):
                dve.sem_inc(drained, RING)
                for s in range(SLOTS):
                    dve.sem_inc(stored[s], 1)
                for s in range(2):
                    dve.sem_inc(v_stored[s], 1)
                dve.sem_inc(v_lo, 2)

                def t_low(n, par, count):
                    dve.wait_ge(t_hi, count + 1)
                    cols = (slice(4 * (n % 2), 4 * (n % 2) + 4), slice((n // 2) * P, (n // 2 + 1) * P))
                    dve.tensor_tensor(xt[par][:, 1, cols[0], cols[1]],
                                      psum[:, n % 2, :].rearrange("p (a t) -> p a t", a=4),
                                      raw(xt[par][:, 0, cols[0], cols[1]]), ALU.subtract).then_inc(t_lo, 1)

                for n in range(NT):
                    t_low(n, 0, n)
                for n in range(w_pieces):
                    dve.wait_ge(w_hi, n + 1)
                    for hi, lo, src, scale in piece(n):
                        done = dve.scalar_tensor_tensor(lo, src, scale, raw(hi), op0=ALU.mult, op1=ALU.subtract)
                    done.then_inc(w_lo, 1)
                dve.wait_ge(w_lo, w_pieces)
                dve.wait_ge(bias_in, 16 * (NQK + 1))
                dve.tensor_scalar(bias_s[:, 0:NQ], bias[:, 0:NQ], SCALE, None, ALU.mult)
                dve.tensor_copy(bias_s[:, NQ:NQK], bias[:, NQ:NQK]).then_inc(bias_scaled, 1)
                dve.wait_ge(bias_scaled, 1)

                def chunk(k, par, t_next):
                    ch = 2 * k + par
                    for n in range(NG):
                        bank = 2 + (NG * par + n) % RING
                        if n < NQK:
                            m = NQK * par + n
                            dve.wait_ge(qk_hi, 2 * NQK * k + m + 1)
                            dve.scalar_tensor_tensor(stage[:, m % SLOTS, 1, :], psum[:, bank, :], bias_s[:, n:n + 1],
                                                     raw(stage[:, m % SLOTS, 0, :]), op0=ALU.add,
                                                     op1=ALU.subtract).then_inc(drained, 1)
                        else:
                            i = n - NQK
                            m = TPC * par + i
                            dve.wait_ge(group_done, 2 * NG * k + NG * par + n + 1)
                            dve.wait_ge(v_lo, 2 * TPC * k + m + 1)
                            dve.tensor_tensor(v_sum[:, i % 2, :], psum[:, bank, 0:KV], bias_v[:, :],
                                              ALU.add).then_inc(drained, 1)
                        if 0 <= n - TURN0 < NT and t_next:
                            t_low(n - TURN0, 1 - par, NT * ch + NT + n - TURN0)

                with dve.Fori(0, NCH // 2 - 1) as k:
                    chunk(k, 0, True)
                    chunk(k, 1, True)
                chunk(NCH // 2 - 1, 0, True)
                chunk(NCH // 2 - 1, 1, False)

            @block.gpsimd
            def _(pool):
                with pool.Fori(0, NCH) as ch:
                    for i in range(TPC):
                        pool.wait_ge(v_hi, TPC * ch + i + 1)
                        pool.tensor_tensor(v_out[:, i % 2, :, 1, :],
                                           v_sum[:, i % 2, :].rearrange("p (g d) -> p g d", d=HD),
                                           raw(v_out[:, i % 2, :, 0, :]), ALU.subtract).then_inc(v_lo, 1)

            @block.tensor
            def _(pe):
                def turn(n, ch):
                    i = n // 2
                    if n % 2 == 0:
                        pe.wait_ge(x_in[i], 16 * (ch + 1))
                    if not (isinstance(ch, int) and NT * ch + n < 2):
                        pe.wait_ge(t_lo, NT * ch + n - 1)
                    for a in range(4):
                        e = 4 * (n % 2) + a
                        done = pe.transpose(psum[:, n % 2, a * P:(a + 1) * P], x_raw[:, i, e * P:(e + 1) * P],
                                            const.ident[:, :])
                    done.then_inc(t_done, 1)

                for n in range(NT):
                    turn(n, 0)

                def chunk(k, par, t_next):
                    ch = 2 * k + par
                    pe.wait_ge(t_lo, NT * ch + NT)
                    for n in range(NG):
                        bank = 2 + (NG * par + n) % RING
                        pe.wait_ge(drained, 2 * NG * k + NG * par + n + 1)
                        if n < NQ and par == 0:
                            pe.wait_ge(w_lo, NKV + n + 1)
                        for e in range(KC):
                            for zw, zx in ((0, 0), (0, 1), (1, 0)):
                                first, last = e == 0 and zw + zx == 0, e == KC - 1 and zw == 1
                                if n < NQ:
                                    out, lhs, rhs = psum[:, bank, :], wq[:, zw, e, n * P:(n + 1) * P], xt[par][:, zx, e, :]
                                elif n < NQK:
                                    o = (n - NQ) * P
                                    out, lhs, rhs = psum[:, bank, :], wk[:, zw, e, o:o + P], xt[par][:, zx, e, :]
                                else:
                                    o = (n - NQK) * P
                                    out, lhs, rhs = psum[:, bank, 0:KV], xt[par][:, zx, e, o:o + P], wv[:, zw, e, :]
                                done = pe.matmul(out, lhs, rhs, start=first, stop=last)
                        done.then_inc(group_done, 1)
                        if 0 <= n - TURN0 < NT and t_next:
                            turn(n - TURN0, ch + 1)

                with pe.Fori(0, NCH // 2 - 1) as k:
                    chunk(k, 0, True)
                    chunk(k, 1, True)
                chunk(NCH // 2 - 1, 0, True)
                chunk(NCH // 2 - 1, 1, False)


def stage_b(nc, dims, dram, const, psum):
    G, HD, S, B = dims.G, dims.HD, dims.S, dims.B
    R = dims.H // G
    NT = S // P
    STEPS = 2 * NT
    ROWS = STEPS * R
    BLOCKS = NT * (NT + 1)
    ROW_LEAD, TURN_LEAD, PV_LEAD = 16, 5, 2
    PART_COST = 256
    PTR = 4
    S_BANKS, T_BANK, O_BANK = 4, 4, 6
    LOOPS = B * G // 2
    PROBS = BLOCKS // 2
    TILES = [t for i in range(NT // 2) for t in (i, NT - 1 - i)]
    assert R * P == 512 and BLOCKS % PTR == 0 and PTR > TURN_LEAD - PV_LEAD and PV_LEAD >= 2

    def tile_of(step):
        return TILES[step % NT]

    def key_blocks(step):
        return tile_of(step) + 1

    def first_block(step):
        return step // STEPS * BLOCKS + sum(key_blocks(t) for t in range(step % STEPS))

    def step_of(block):
        return next(t for t in range(block // BLOCKS * STEPS, (block // BLOCKS + 1) * STEPS)
                    if first_block(t) <= block < first_block(t + 1))

    def row_banks(row):
        def banks(r):
            return 1 if key_blocks(r // R) * P <= 512 else 2
        return sum(banks(r) for r in range(row % ROWS)) % S_BANKS, banks(row)

    def row_before(row, part):
        at = row_banks(row)[0] + part
        r = row - 1
        while at not in range(row_banks(r % ROWS)[0], sum(row_banks(r % ROWS))):
            r -= 1
        return r

    def group_parts():
        parts = [(row, part) for row in range(R * NT) for part in range(row_banks(row)[1])]
        costs = [key_blocks(row // R) * P // row_banks(row)[1] + PART_COST for row, _ in parts]
        ends = {}
        for group in range(2):
            out, last = [], 0
            for n, (row, part) in enumerate(parts):
                before = ends.get(R * NT * group + row_before(R * NT + row, part) - R * NT, -ROW_LEAD)
                last = max(last, before + 2, BLOCKS // 2 * group + sum(costs[:n]) * (BLOCKS // 2) // sum(costs))
                ends[R * NT * group + row] = last
                out.append((row, part, last - BLOCKS // 2 * group))
        return out

    def parts_at(i):
        return [(R * NT * g + row, part) for g in range(3) for row, part, at in GROUP_PARTS
                if BLOCKS // 2 * g + at - ROW_LEAD == i]

    GROUP_PARTS = group_parts()
    assert (NT - 2) % 3 == 0 and {TILES[0], TILES[1]} == {0, NT - 1} and first_block(2) < ROW_LEAD
    assert all(at - ROW_LEAD + 2 <= first_block(row // R) - TURN_LEAD for row, _, at in GROUP_PARTS)
    PARTS_AT = {i: parts_at(i) for i in range(-ROW_LEAD, BLOCKS)}

    def ends_row(row, part):
        return part == row_banks(row)[1] - 1

    def exps_at(i):
        early, rest = [], []
        for row, part in PARTS_AT.get(i, []):
            while rest and rest[0] <= row_before(row, part):
                early.append(rest.pop(0))
            if ends_row(row, part):
                rest.append(row)
        return early, rest

    def positions(part):
        for i in range(-ROW_LEAD, 0) if part == "prologue" else range(BLOCKS):
            end = 1 if part == "last" else 2
            parts = [(r, p) for r, p in PARTS_AT[i] if r < end * ROWS]
            turn, pv = (x if 0 <= x < end * BLOCKS else None for x in (i + TURN_LEAD, i + PV_LEAD))
            copy = [s for s in range(end * STEPS) if first_block(s + 1) - 2 == i]
            out = [s for s in range(end * STEPS) if min(first_block(s + 1), first_block(s + 2) - PV_LEAD) == i]
            yield i, parts, turn, pv, copy, out

    with ExitStack() as c:
        def sb(name, shape, dt=F32):
            return c.enter_context(nc.sbuf_tensor(name, shape, dt))

        def sem(name):
            return c.enter_context(nc.semaphore(name))

        q = sb("q_sb", [P, 2, R, S], F32R)
        kk = sb("k_sb", [P, 2, 2, S], F32R)
        v = sb("v_sb", [P, 2, NT, 2 * HD], F32R)
        probs = sb("probs", [P, PROBS * R * P])
        pt = sb("pt", [P, PTR, 2, R * P], F32R)
        top = sb("top", [P, ROWS])
        sums = sb("sums", [P, ROWS])
        inv = sb("inv", [P, 2, R])
        o_t = sb("o_t", [P, 2, R * P])
        res = sb("res", [P, 2, R, HD])
        qk_in = [sem(f"b_qk_in{i}") for i in range(2)]
        first_in = [sem(f"b_first_in{i}") for i in range(2)]
        v_in = [sem(f"b_v_in{i}") for i in range(2)]
        scored, topped, expd = sem("b_scored"), sem("b_topped"), sem("b_expd")
        turned, hi_done, lo_done = sem("b_turned"), sem("b_hi_done"), sem("b_lo_done")
        pv_done = sem("b_pv_done")
        o_copied, o_turned, inverted = sem("b_o_copied"), sem("b_o_turned"), sem("b_inverted")
        scaled = sem("b_scaled")
        stored = [sem(f"b_stored{i}") for i in range(2)]
        idle = sem("b_idle")

        def row_probs(s, h):
            n = key_blocks(s)
            at = (first_block(s) % PROBS * R + h * n) * P
            return probs[:, at:at + n * P]

        def row_view(ap, n):
            banks = 1 if n * P <= 512 else 2
            return ap[:, :, 0:n * P // banks]

        with nc.Block() as block:

            @block.sync
            def _(sp):
                def load_qk(g, par):
                    sp.dma_start(raw(q[:, par]), dram.q[bass.ds(g, 1)].rearrange("a h p t -> (a p) h t")
                                 ).then_inc(qk_in[par], 16)
                    for half in range(2):
                        sp.dma_start(raw(kk[half * HD:(half + 1) * HD, par]),
                                     dram.k[bass.ds(g, 1)].rearrange("a z p t -> (a p) z t")).then_inc(qk_in[par], 16)

                def load_v(g, par):
                    sp.dma_start(raw(v[:, par]), dram.v[bass.ds(g, 1)].rearrange("a (j p) f -> p (a j) f", p=P)
                                 ).then_inc(v_in[par], 16)

                for half in range(2):
                    sp.dma_start(raw(kk[half * HD:(half + 1) * HD, 0]),
                                 dram.k[0:1].rearrange("a z p t -> (a p) z t")).then_inc(first_in[0], 16)
                q_first = dram.q[0:1].rearrange("a h p t -> (a p) h t")
                rest = (NT - 2) // 3
                for first, n, arrived in [(TILES[0], 1, first_in[0]), (TILES[1], 1, first_in[1])] + \
                        [(1 + rest * i, rest, qk_in[0]) for i in range(3)]:
                    cols = slice(first * P, (first + n) * P)
                    sp.dma_start(raw(q[:, 0, :, cols]), q_first[:, :, cols]).then_inc(arrived, 16)
                load_v(0, 0)
                load_qk(1, 1)
                load_v(1, 1)

                def body(k, last):
                    for s in range(STEPS):
                        gp, tile = s // NT, tile_of(s)
                        sp.wait_ge(scaled, STEPS * k + s + 1 + 2)
                        sp.sem_inc(idle, 1)
                        sp.dma_start(dram.att[bass.ds(k // (G // 2), 1), tile * P:(tile + 1) * P,
                                              bass.ds(2 * (k % (G // 2)) + gp, 1), :].rearrange("a t g n -> t (a g n)"),
                                     res[:, s % 2].rearrange("p h d -> p (h d)")).then_inc(stored[s % 2], 16)
                        if last:
                            continue
                        if s in (NT - 3, STEPS - 3):
                            sp.wait_ge(scored, ROWS * k + R * NT * (1 + s // NT))
                            load_qk(2 * k + 2 + s // NT, s // NT)
                        if s in (NT, STEPS - 1):
                            sp.wait_ge(pv_done, BLOCKS * k + BLOCKS // 2 * (1 + (s > NT)))
                            load_v(2 * k + 2 + (s > NT), int(s > NT))

                for i in range(dims.D // P):
                    sp.dma_start(const.w_raw[:, i, :], dram.wup[i * P:(i + 1) * P, :]).then_inc(const.wup_in, 16)

                with sp.Fori(0, LOOPS - 1) as k:
                    body(k, False)
                body(LOOPS - 1, True)
                for i in range(2):
                    sp.wait_ge(stored[i], 16 * STEPS * LOOPS // 2 + 1)

            @block.tensor
            def _(pe):
                def scores(k, row, part):
                    s, h = row // R, row % R
                    gp, n = s // NT % 2, key_blocks(s)
                    if isinstance(k, int) and k == 0 and s < 3:
                        if h + part == 0:
                            pe.wait_ge([first_in[0], first_in[1], qk_in[0]][s], [48, 16, 48][s])
                    elif s % NT == 0 and h + part == 0:
                        pe.wait_ge(qk_in[gp], 48 * (k + s // STEPS + 1))
                    before = row_before(row, part)
                    if not (isinstance(k, int) and ROWS * k + before < 0):
                        pe.wait_ge(expd, ROWS * k + before + 1)
                    bank, banks = row_banks(row)
                    w = n * P // banks
                    lhs = q[:, gp, h, tile_of(s) * P:(tile_of(s) + 1) * P]
                    keys = slice(part * w, (part + 1) * w)
                    out = psum[:, bank + part, 0:w]
                    pe.matmul(out, lhs, kk[:, gp, 0, keys], start=True, stop=False)
                    if keys.stop == n * P:
                        pe.matmul(out[:, w - P:w], const.ident_r[:, :], const.mask[:, :], start=False, stop=False)
                    done = pe.matmul(out, lhs, kk[:, gp, 1, keys], start=False, stop=True)
                    if ends_row(row, part):
                        done.then_inc(scored, 1)

                def turn(k, b):
                    s = step_of(b)
                    j = b - first_block(s)
                    if j == 0:
                        pe.wait_ge(expd, ROWS * k + R * (s + 1))
                    if not (isinstance(k, int) and BLOCKS * k + b < 2):
                        pe.wait_ge(lo_done, BLOCKS * k + b - 1)
                    for h in range(R):
                        done = pe.transpose(psum[:, T_BANK + b % 2, h * P:(h + 1) * P],
                                            row_probs(s, h)[:, j * P:(j + 1) * P], const.ident[:, :])
                    done.then_inc(turned, 1)

                def times_v(k, b):
                    s = step_of(b)
                    j, gp = b - first_block(s), s // NT % 2
                    if j == 0:
                        if s % NT == 0:
                            pe.wait_ge(v_in[gp], 16 * (k + s // STEPS + 1))
                        if not (isinstance(k, int) and STEPS * k + s < 2):
                            pe.wait_ge(scaled, STEPS * k + s - 1 + 2)
                    pe.wait_ge(lo_done, BLOCKS * k + b + 1)
                    for z in range(2):
                        done = pe.matmul(psum[:, O_BANK + s % 2, :], v[:, gp, j, :], pt[:, b % PTR, z, :],
                                         start=j == 0 and z == 0, stop=j == key_blocks(s) - 1 and z == 1)
                    done.then_inc(pv_done, 1)

                def turn_out(k, s):
                    pe.wait_ge(o_copied, STEPS * k + s + 1)
                    for h in range(R):
                        done = pe.matmul(psum[:, O_BANK + s % 2, h * HD:(h + 1) * HD], o_t[:, s % 2, h * P:(h + 1) * P],
                                         const.fold[:, :], start=True, stop=True)
                    done.then_inc(o_turned, 1)

                def run(k, part):
                    for i, parts, block_t, block_v, _, out in positions(part):
                        for s in out:
                            turn_out(k, s)
                        if block_t is not None:
                            turn(k, block_t)
                        for row, bank in parts:
                            scores(k, row, bank)
                        if block_v is not None:
                            times_v(k, block_v)

                run(0, "prologue")
                with pe.Fori(0, LOOPS - 1) as k:
                    run(k, "body")
                run(LOOPS - 1, "last")

            @block.scalar
            def _(act):
                def exp(k, row):
                    s, h = row // R, row % R
                    n = key_blocks(s)
                    bank, banks = row_banks(row)
                    act.wait_ge(topped, ROWS * k + row + 1)
                    at = row % ROWS
                    act.activation(row_probs(s, h).rearrange("p (a w) -> p a w", a=banks),
                                   row_view(psum[:, bank:bank + banks, :], n), ACT.Exp, bias=top[:, at:at + 1],
                                   accum_out=sums[:, at:at + 1]).then_inc(expd, 1)

                def run(k, part):
                    for i, _, b, _, copy, _ in positions(part):
                        for s in copy:
                            act.wait_ge(pv_done, BLOCKS * k + first_block(s + 1))
                            act.activation(o_t[:, s % 2, :], psum[:, O_BANK + s % 2, :], ACT.Copy).then_inc(o_copied, 1)
                        if b is not None:
                            act.wait_ge(turned, BLOCKS * k + b + 1)
                            act.activation(pt[:, b % PTR, 0, :], psum[:, T_BANK + b % 2, :], ACT.Copy).then_inc(hi_done, 1)
                        for row in exps_at(i - 1)[1] + exps_at(i)[0]:
                            if part != "last" or row < ROWS:
                                exp(k, row)

                run(0, "prologue")
                with act.Fori(0, LOOPS - 1) as k:
                    run(k, "body")
                run(LOOPS - 1, "last")

            @block.vector
            def _(dve):
                dve.sem_inc(scaled, 2)
                for i in range(2):
                    dve.sem_inc(stored[i], 1)

                def maximum(k, row):
                    bank, banks = row_banks(row)
                    at = row % ROWS
                    dve.wait_ge(scored, ROWS * k + row + 1)
                    dve.tensor_reduce(top[:, at:at + 1], row_view(psum[:, bank:bank + banks, :], key_blocks(row // R)),
                                      AX.XY, ALU.max, negate=True).then_inc(topped, 1)

                def run(k, part):
                    for i, parts, b, _, copy, out in positions(part):
                        for s in out:
                            at = s % 2
                            dve.wait_ge(inverted, STEPS * k + s + 1)
                            dve.wait_ge(stored[at], 16 * (STEPS // 2 * k + s // 2) + 1)
                            dve.wait_ge(o_turned, STEPS * k + s + 1)
                            dve.tensor_tensor(res[:, at], psum[:, O_BANK + at, 0:R * HD].rearrange("p (h d) -> p h d", d=HD),
                                              inv[:, at, :, None].broadcast_to([P, R, HD]), ALU.mult).then_inc(scaled, 1)
                        for row in [r for r, p in parts if ends_row(r, p)]:
                            maximum(k, row)
                        if b is not None:
                            dve.wait_ge(hi_done, BLOCKS * k + b + 1)
                            dve.tensor_tensor(pt[:, b % PTR, 1, :], psum[:, T_BANK + b % 2, :],
                                              raw(pt[:, b % PTR, 0, :]), ALU.subtract).then_inc(lo_done, 1)
                        for s in copy:
                            dve.wait_ge(scaled, STEPS * k + s + 1)
                            dve.wait_ge(expd, ROWS * k + R * (s + 1))
                            dve.reciprocal(inv[:, s % 2, :], sums[:, s % STEPS * R:(s % STEPS + 1) * R]
                                           ).then_inc(inverted, 1)

                run(0, "prologue")
                with dve.Fori(0, LOOPS - 1) as k:
                    run(k, "body")
                run(LOOPS - 1, "last")


def stage_c(nc, dims, dram, const, psum):
    D, G, S, B, E = dims.D, dims.G, dims.S, dims.B, dims.E
    KC = D // P
    TPC = 2
    CH = TPC * P
    NCH = B * S // CH
    LOOPS = NCH // 2
    CPB = S // CH
    NT = 2 * TPC
    XR = 2 * TPC + 2
    UP_BANKS = 2
    W_BANKS = 8
    WX = D + E
    EB = 3
    EN = WX // EB
    GATE_BANK, GATE_COL = EB - 1, D - (EB - 1) * EN
    assert WX % EB == 0 and EN <= 512 and EN % 2 == 0
    with ExitStack() as c:
        def sb(name, shape, dt=F32):
            return c.enter_context(nc.sbuf_tensor(name, shape, dt))

        def sem(name):
            return c.enter_context(nc.semaphore(name))

        wup = sb("wup_t", [P, 2, KC, D], F32R)
        wex = sb("wex", [P, 2, KC, WX], F32R)
        yt = const.yt
        y = sb("y", [P, 2 * TPC, D])
        att = const.att
        h_out = sb("h_out", [P, 4, CH])
        stats = sb("stats", [P, 2, 2, 6])
        mv = sb("mv", [P, 2 * TPC, 2])
        std = sb("std", [P, 2 * TPC])
        rstd = sb("rstd", [P, 2 * TPC])
        eps = sb("eps_c", [P, 1])
        best = sb("best", [P, 2 * TPC, 8])
        nbest = sb("nbest", [P, 2 * TPC])
        ex = sb("ex", [P, 2 * TPC, 2])
        ex_sum = sb("ex_sum", [P, 2 * TPC])
        ex_inv = sb("ex_inv", [P, 2 * TPC])
        route = sb("route", [P, 2 * TPC, 2])
        route_sum = sb("route_sum", [P, 2 * TPC])
        idle = sem("c_idle")
        gate_in = sem("c_gate_in")
        w_in = [sem(f"c_w_in{i}") for i in range(KC)]
        w_zero = sem("c_w_zero")
        w_turned, w_hi, w_lo = sem("c_w_turned"), sem("c_w_hi"), sem("c_w_lo")
        x_in = [sem(f"c_x_in{i}") for i in range(2 * TPC)]
        att_in = [sem(f"c_att_in{i}") for i in range(2)]
        chain = sem("c_chain")
        var_done, std_done = sem("c_var_done"), sem("c_std_done")
        y_done = sem("c_y_done")
        turned, t_hi, t_lo = sem("c_turned"), sem("c_t_hi"), sem("c_t_lo")
        up_done = sem("c_up_done")
        relu_done = sem("c_relu_done")
        h_stored = [sem(f"c_h_stored{i}") for i in range(4)]
        exp_done_pe = sem("c_expert_done")
        e_free = sem("c_e_free")
        nbest_done, soft_done = sem("c_nbest_done"), sem("c_soft_done")
        r_done = sem("c_r_done")
        r_stored = [sem(f"c_r_stored{i}") for i in range(2 * TPC)]

        EB_ORDER = [GATE_BANK] + [b for b in range(EB) if b != GATE_BANK]
        E_BANK0 = 2 + UP_BANKS

        gate_raw = h_out.rearrange("p a t -> p (a t)")

        def wex_raw(e):
            return const.w_raw[:, KC // 2 + e - 2, :] if 2 <= e < 6 else y[:, 2 + e % 2, :]

        turn_groups = 2 * KC + 2

        with nc.Block() as block:

            @block.sync
            def _(sp):
                def load(k, t):
                    tile = 2 * TPC * k + t
                    sp.dma_start(y[:, t, :], dram.x[bass.ds(tile, 1)].rearrange("a p n -> (a p) n")
                                 ).then_inc(x_in[t], 16)
                    sp.dma_start(att[:, t % 2, :], dram.att_tiles[bass.ds(tile, 1)].rearrange("a p n -> (a p) n")
                                 ).then_inc(att_in[t % 2], 16)

                def load_wex(e):
                    sp.dma_start(wex_raw(e), dram.wex[e * P:(e + 1) * P, :]).then_inc(w_in[e], 16)

                sp.wait_ge(w_zero, 1)
                sp.dma_start(gate_raw[0:E, :], dram.wg[:, :]).then_inc(gate_in, 16)
                load(0, 0)
                load(0, 1)
                load_wex(0)
                load_wex(1)
                sp.wait_ge(w_turned, 2 * KC)
                for e in range(2, 6):
                    load_wex(e)
                for e in range(6, KC):
                    sp.wait_ge(w_lo, turn_groups + e - 6 + 1)
                    load_wex(e)
                for t in range(2, 2 * TPC):
                    sp.wait_ge(w_lo, turn_groups + 6 + t - 1)
                    sp.wait_ge(y_done, t - 1)
                    load(0, t)

                def chunk(k, par, loads):
                    ch = 2 * k + par
                    for n in range(KC):
                        sp.wait_ge(relu_done, KC * ch + n + 1 + UP_BANKS)
                        sp.dma_start(dram.h[bass.ds(TPC * ch, TPC), :, n, :].rearrange("a p t -> p a t"),
                                     h_out[:, n % 4, :].rearrange("p (a t) -> p a t", a=TPC)).then_inc(h_stored[n % 4], 16)
                    for i in range(TPC):
                        t = TPC * par + i
                        sp.wait_ge(e_free, EB * (TPC * ch + i + 1) + EB)
                        sp.dma_start(dram.r[bass.ds(2 * TPC * k + t, 1)].rearrange("a p n -> (a p) n"), y[:, t, :]
                                     ).then_inc(r_stored[t], 16)
                    for i in range(TPC if loads else 0):
                        t = TPC * par + i
                        sp.wait_ge(r_stored[t], 16 * (k + 1))
                        sp.wait_ge(y_done, TPC * (ch + 2))
                        load(k + 1, t)

                with sp.Fori(0, LOOPS - 1) as k:
                    chunk(k, 0, True)
                    chunk(k, 1, True)
                chunk(LOOPS - 1, 0, False)
                sp.wait_ge(exp_done_pe, TPC * EB * (NCH - 1))
                sp.wait_ge(y_done, TPC * NCH)
                for i in range(6):
                    sp.dma_start(wdown_raw(const, i), dram.wdown[i * P:(i + 1) * P, :]).then_inc(const.wdown_in, 16)
                chunk(LOOPS - 1, 1, False)
                for i in range(4):
                    sp.wait_ge(h_stored[i], 16 * KC * NCH // 4 + 1)
                for t in range(2 * TPC):
                    sp.wait_ge(r_stored[t], 16 * LOOPS)

            @block.gpsimd
            def _(pool):
                pool.memset(gate_raw, 0.0).then_inc(w_zero, 1)

            @block.tensor
            def _(pe):
                for n in range(turn_groups):
                    i, half = n // 2, n % 2
                    if n == 0:
                        pe.wait_ge(const.wup_in, 16 * KC)
                    if n == 2 * KC:
                        pe.wait_ge(gate_in, 16)
                    if n >= W_BANKS:
                        pe.wait_ge(w_lo, n - W_BANKS + 1)
                    src = const.w_raw[:, i, :] if i < KC else gate_raw
                    for a in range(4):
                        e = 4 * half + a
                        done = pe.transpose(psum[:, n % W_BANKS, a * P:(a + 1) * P], src[:, e * P:(e + 1) * P],
                                            const.ident[:, :])
                    done.then_inc(w_turned, 1)

                def turn(ch, par, n):
                    i, half = n // 2, n % 2
                    pe.wait_ge(y_done, TPC * ch + i + 1)
                    if isinstance(ch, int) and NT * ch + n < 2:
                        pe.wait_ge(w_lo, turn_groups)
                    else:
                        pe.wait_ge(t_lo, NT * ch + n - 1)
                    for a in range(4):
                        e = 4 * half + a
                        done = pe.transpose(psum[:, n % 2, a * P:(a + 1) * P], y[:, TPC * par + i, e * P:(e + 1) * P],
                                            const.ident[:, :])
                    done.then_inc(turned, 1)

                for n in range(NT):
                    turn(0, 0, n)

                def chunk(k, par, more):
                    ch = 2 * k + par
                    pe.wait_ge(t_lo, NT * (ch + 1))
                    for n in range(KC):
                        pe.wait_ge(relu_done, KC * ch + n + 1)
                        for e in range(KC):
                            for zw, zx in ((0, 0), (0, 1), (1, 0)):
                                done = pe.matmul(psum[:, 2 + n % UP_BANKS, 0:CH], wup[:, zw, e, n * P:(n + 1) * P],
                                                 yt[par][:, zx, e, :], start=e == 0 and zw + zx == 0,
                                                 stop=e == KC - 1 and zw == 1)
                        done.then_inc(up_done, 1)
                    if par == 0:
                        pe.wait_ge(w_lo, turn_groups + KC)
                    for m in range(TPC * EB):
                        i, b = m // EB, EB_ORDER[m % EB]
                        pe.wait_ge(e_free, TPC * EB * ch + m + 1)
                        for e in range(KC):
                            for zw, zx in ((0, 0), (0, 1), (1, 0)):
                                done = pe.matmul(psum[:, E_BANK0 + b, 0:EN], yt[par][:, zx, e, i * P:(i + 1) * P],
                                                 wex[:, zw, e, b * EN:(b + 1) * EN], start=e == 0 and zw + zx == 0,
                                                 stop=e == KC - 1 and zw == 1)
                        done.then_inc(exp_done_pe, 1)
                        if more and 1 <= m <= NT:
                            turn(ch + 1, 1 - par, m - 1)

                with pe.Fori(0, LOOPS - 1) as k:
                    chunk(k, 0, True)
                    chunk(k, 1, True)
                chunk(LOOPS - 1, 0, True)
                chunk(LOOPS - 1, 1, False)

            @block.scalar
            def _(act):
                for n in range(turn_groups):
                    i, half = n // 2, n % 2
                    act.wait_ge(w_turned, n + 1)
                    src = psum[:, n % W_BANKS, :].rearrange("p (a t) -> p a t", a=4)
                    dst = wup[:, 0, 4 * half:4 * half + 4, i * P:(i + 1) * P] if i < KC else \
                        wex[:, 0, 4 * half:4 * half + 4, D:WX]
                    act.activation(dst, src if i < KC else src[:, :, 0:E], ACT.Copy).then_inc(w_hi, 1)
                def root(ch, par):
                    act.wait_ge(var_done, TPC * (ch + 1))
                    act.activation(std[:, TPC * par:TPC * par + TPC], mv[:, TPC * par:TPC * par + TPC, 1], ACT.Sqrt,
                                   bias=eps[:, 0:1]).then_inc(std_done, 1)

                def t_high(ch, par, n):
                    i, half = n // 2, n % 2
                    act.wait_ge(turned, NT * ch + n + 1)
                    act.activation(yt[par][:, 0, 4 * half:4 * half + 4, i * P:(i + 1) * P],
                                   psum[:, n % 2, :].rearrange("p (a t) -> p a t", a=4), ACT.Copy).then_inc(t_hi, 1)

                root(0, 0)
                for n in range(NT):
                    t_high(0, 0, n)
                for e in range(KC):
                    act.wait_ge(w_in[e], 16)
                    act.activation(wex[:, 0, e, 0:D], wex_raw(e), ACT.Copy).then_inc(w_hi, 1)
                act.wait_ge(w_lo, turn_groups + 6)

                def chunk(k, par, more):
                    ch = 2 * k + par
                    for n in range(KC):
                        act.wait_ge(up_done, KC * ch + n + 1)
                        act.wait_ge(h_stored[n % 4], 16 * (KC // 4 * ch + n // 4) + 1)
                        act.activation(h_out[:, n % 4, :], psum[:, 2 + n % UP_BANKS, 0:CH], ACT.Relu
                                       ).then_inc(relu_done, 1)
                        if n == 5 and more:
                            root(ch + 1, 1 - par)
                    for m in range(TPC * EB):
                        i, t = m // EB, TPC * par + m // EB
                        if m % EB == 0:
                            act.wait_ge(nbest_done, TPC * ch + i + 1)
                            act.activation(ex[:, t, :], best[:, t, 0:2], ACT.Exp, bias=nbest[:, t:t + 1],
                                           accum_out=ex_sum[:, t:t + 1]).then_inc(soft_done, 1)
                        if more and 1 <= m <= NT:
                            t_high(ch + 1, 1 - par, m - 1)

                with act.Fori(0, LOOPS - 1) as k:
                    chunk(k, 0, True)
                    chunk(k, 1, True)
                chunk(LOOPS - 1, 0, True)
                chunk(LOOPS - 1, 1, False)

            @block.vector
            def _(dve):
                dve.memset(eps[:, :], EPS).then_inc(chain, 1)
                dve.sem_inc(relu_done, UP_BANKS)
                dve.sem_inc(e_free, EB)
                for i in range(4):
                    dve.sem_inc(h_stored[i], 1)
                for n in range(turn_groups):
                    i, half = n // 2, n % 2
                    dve.wait_ge(w_hi, n + 1)
                    src = psum[:, n % W_BANKS, :].rearrange("p (a t) -> p a t", a=4)
                    dst = wup[:, :, 4 * half:4 * half + 4, i * P:(i + 1) * P] if i < KC else \
                        wex[:, :, 4 * half:4 * half + 4, D:WX]
                    dve.tensor_tensor(dst[:, 1], src if i < KC else src[:, :, 0:E], raw(dst[:, 0]), ALU.subtract
                                      ).then_inc(w_lo, 1)
                LINKS = 7
                STEP = LINKS + 3 * TPC

                def norm(k, ch, par, base):
                    for i in range(TPC):
                        t = TPC * par + i
                        dve.wait_ge(x_in[t], 16 * (k + 1))
                        dve.wait_ge(att_in[t % 2], 16 * (2 * k + t // 2 + 1))
                        dve.tensor_tensor(y[:, t, :], y[:, t, :], att[:, t % 2, :], ALU.add).then_inc(chain, 1)
                    for i in range(TPC):
                        t = TPC * par + i
                        dve.wait_ge(chain, base + i + 1)
                        for half in range(2):
                            dve.bn_stats(stats[:, i, half, :], y[:, t, half * 512:(half + 1) * 512]).then_inc(chain, 1)
                    dve.wait_ge(chain, base + TPC + 2 * TPC)
                    dve.sem_inc(idle, 1)
                    for i in range(TPC):
                        t = TPC * par + i
                        dve.bn_aggr(mv[:, t, :], stats[:, i].rearrange("p a b -> p (a b)")).then_inc(var_done, 1)
                    dve.wait_ge(std_done, ch + 1)
                    dve.reciprocal(rstd[:, TPC * par:TPC * par + TPC], std[:, TPC * par:TPC * par + TPC]
                                   ).then_inc(chain, 1)
                    dve.wait_ge(chain, base + LINKS)
                    for i in range(TPC):
                        t = TPC * par + i
                        dve.tensor_scalar(y[:, t, :], y[:, t, :], mv[:, t, 0:1], rstd[:, t:t + 1], ALU.subtract,
                                          ALU.mult).then_inc(y_done, 1)

                def t_low(ch, par, n):
                    i, half = n // 2, n % 2
                    dve.wait_ge(t_hi, NT * ch + n + 1)
                    at = yt[par][:, :, 4 * half:4 * half + 4, i * P:(i + 1) * P]
                    dve.tensor_tensor(at[:, 1], psum[:, n % 2, :].rearrange("p (a t) -> p a t", a=4), raw(at[:, 0]),
                                      ALU.subtract).then_inc(t_lo, 1)

                norm(0, 0, 0, 1)
                for n in range(NT):
                    t_low(0, 0, n)
                for e in range(KC):
                    dve.wait_ge(w_hi, turn_groups + e + 1)
                    dve.tensor_tensor(wex[:, 1, e, 0:D], wex_raw(e), raw(wex[:, 0, e, 0:D]),
                                      ALU.subtract).then_inc(w_lo, 1)

                def chunk(k, par, more):
                    ch = 2 * k + par
                    base = 1 + LINKS + STEP * ch
                    if more:
                        norm(k + par, ch + 1, 1 - par, base)
                    base = base + (LINKS if more else 0)
                    for m in range(TPC * EB):
                        i, t, b = m // EB, TPC * par + m // EB, EB_ORDER[m % EB]
                        dve.wait_ge(exp_done_pe, TPC * EB * ch + m + 1)
                        if m % EB == 0:
                            dve.sem_inc(idle, 1)
                            dve.max(best[:, t, :], psum[:, E_BANK0 + b, GATE_COL:GATE_COL + E]).then_inc(chain, 1)
                            dve.wait_ge(chain, base + 3 * i + 1)
                            dve.tensor_scalar(nbest[:, t:t + 1], best[:, t, 0:1], -1.0, None, ALU.mult
                                              ).then_inc(nbest_done, 1)
                            dve.wait_ge(soft_done, TPC * ch + i + 1)
                            dve.reciprocal(ex_inv[:, t:t + 1], ex_sum[:, t:t + 1]).then_inc(chain, 1)
                            dve.wait_ge(chain, base + 3 * i + 2)
                            dve.tensor_scalar(route[:, t, :], ex[:, t, :], ex_inv[:, t:t + 1], 0.0, ALU.mult, ALU.add,
                                              accum_out=route_sum[:, t:t + 1]).then_inc(chain, 1)
                            dve.wait_ge(chain, base + 3 * i + 3)
                        w = EN if b < EB - 1 else GATE_COL
                        cols = slice(b * EN, b * EN + w)
                        dve.scalar_tensor_tensor(y[:, t, cols], psum[:, E_BANK0 + b, 0:w], route_sum[:, t:t + 1],
                                                 y[:, t, cols], op0=ALU.mult, op1=ALU.add).then_inc(e_free, 1)
                        if more and 1 <= m <= NT:
                            t_low(ch + 1, 1 - par, m - 1)

                with dve.Fori(0, LOOPS - 1) as k:
                    chunk(k, 0, True)
                    chunk(k, 1, True)
                chunk(LOOPS - 1, 0, True)
                chunk(LOOPS - 1, 1, False)


def stage_d(nc, dims, dram, const, psum):
    D, S, B = dims.D, dims.S, dims.B
    KC = D // P
    NTILES = B * S // P
    TB = 4
    LOOPS = NTILES // TB
    HALVES, HW = 2, D // 2
    turn_groups = 2 * KC
    W_BANKS = 8
    with ExitStack() as c:
        def sb(name, shape, dt=F32):
            return c.enter_context(nc.sbuf_tensor(name, shape, dt))

        def sem(name):
            return c.enter_context(nc.semaphore(name))

        wd = sb("wdown_t", [P, 2, KC, D], F32R)
        w_late = sb("w_raw_d", [P, 2, D])
        h_raw = sb("h_raw", [P, 2, KC, P])
        ht = sb("ht", [P, 2, 2, KC, P], F32R)
        r = sb("r_sb", [P, TB, D])
        stats = sb("stats_d", [P, 2, HALVES, 6])
        mv = sb("mv_d", [P, 2, 2])
        std = sb("std_d", [P, 2])
        rstd = sb("rstd_d", [P, 2])
        eps = sb("eps_d", [P, 1])
        idle = sem("d_idle")
        w_in = sem("d_w_in")
        w_turned, w_hi, w_lo = sem("d_w_turned"), sem("d_w_hi"), sem("d_w_lo")
        h_in = [sem(f"d_h_in{i}") for i in range(2)]
        r_in = [sem(f"d_r_in{i}") for i in range(TB)]
        h_hi, h_lo = sem("d_h_hi"), sem("d_h_lo")
        done_half = sem("d_done_half")
        added = sem("d_added")
        counted, var_done, std_done, inverted = sem("d_counted"), sem("d_var_done"), sem("d_std_done"), sem("d_inverted")
        normed = sem("d_normed")
        eps_set = sem("d_eps_set")
        stored = [sem(f"d_stored{i}") for i in range(TB)]
        BANK0 = 2

        with nc.Block() as block:

            @block.sync
            def _(sp):
                def load_h(tile, par):
                    sp.dma_start(h_raw[:, par], dram.h[bass.ds(tile, 1)].rearrange("a p n t -> (a p) n t")
                                 ).then_inc(h_in[par], 16)

                def load_r(tile, t):
                    sp.dma_start(r[:, t, :], dram.r[bass.ds(tile, 1)].rearrange("a p n -> (a p) n")
                                 ).then_inc(r_in[t], 16)

                for i in range(6, KC):
                    sp.dma_start(w_late[:, i - 6, :], dram.wdown[i * P:(i + 1) * P, :]).then_inc(w_in, 16)
                for t in range(2):
                    load_h(t, t)
                for t in range(TB - 1):
                    load_r(t, t)
                sp.wait_ge(h_lo, 1)
                load_h(2, 0)

                def step(k, t, more_h, more_r, first):
                    if more_h:
                        sp.wait_ge(h_lo, TB * k + t + 2)
                        load_h(TB * k + t + 3, (t + 1) % 2)
                    sp.wait_ge(normed, TB * k + t + 1)
                    sp.dma_start(dram.out[bass.ds(TB * k + t, 1)].rearrange("a p n -> (a p) n"), r[:, t, :]
                                 ).then_inc(stored[t], 16)
                    if more_r:
                        if t >= 1:
                            sp.wait_ge(stored[t - 1], 16 * (k + 1))
                        elif not first:
                            sp.wait_ge(stored[TB - 1], 16 * k)
                        load_r(TB * k + t + TB - 1, (t + TB - 1) % TB)

                for t in range(TB):
                    step(0, t, True, True, True)
                with sp.Fori(1, LOOPS - 1) as k:
                    for t in range(TB):
                        step(k, t, True, True, False)
                for t in range(TB):
                    step(LOOPS - 1, t, t + 3 < TB, t + TB - 1 < TB, False)
                for t in range(TB):
                    sp.wait_ge(stored[t], 16 * LOOPS)

            @block.tensor
            def _(pe):
                for n in range(turn_groups):
                    i, half = n // 2, n % 2
                    if n == 0:
                        pe.wait_ge(const.wdown_in, 16 * 6)
                    if n == 2 * 6:
                        pe.wait_ge(w_in, 16 * (KC - 6))
                    if n >= W_BANKS:
                        pe.wait_ge(w_lo, n - W_BANKS + 1)
                    src = wdown_raw(const, i) if i < 6 else w_late[:, i - 6, :]
                    for a in range(4):
                        e = 4 * half + a
                        done = pe.transpose(psum[:, n % W_BANKS, a * P:(a + 1) * P], src[:, e * P:(e + 1) * P],
                                            const.ident[:, :])
                    done.then_inc(w_turned, 1)
                pe.wait_ge(w_lo, turn_groups)
                with pe.Fori(0, LOOPS) as k:
                    for t in range(TB):
                        par = t % 2
                        pe.wait_ge(h_lo, TB * k + t + 1)
                        for half in range(HALVES):
                            bank = BANK0 + HALVES * par + half
                            pe.wait_ge(added, HALVES * (TB * k + t) + half + 1)
                            for e in range(KC):
                                for zh, zw in ((0, 0), (0, 1), (1, 0)):
                                    done = pe.matmul(psum[:, bank, :], ht[:, par, zh, e, :],
                                                     wd[:, zw, e, half * HW:(half + 1) * HW],
                                                     start=e == 0 and zh + zw == 0, stop=e == KC - 1 and zh == 1)
                            done.then_inc(done_half, 1)

            @block.scalar
            def _(act):
                for n in range(turn_groups):
                    i, half = n // 2, n % 2
                    act.wait_ge(w_turned, n + 1)
                    act.activation(wd[:, 0, 4 * half:4 * half + 4, i * P:(i + 1) * P],
                                   psum[:, n % W_BANKS, :].rearrange("p (a t) -> p a t", a=4), ACT.Copy
                                   ).then_inc(w_hi, 1)

                def high(k, t):
                    act.wait_ge(h_in[t % 2], 16 * (TB // 2 * k + t // 2 + 1))
                    if not (isinstance(k, int) and TB * k + t < 2):
                        act.wait_ge(done_half, HALVES * (TB * k + t - 1))
                    act.activation(ht[:, t % 2, 0], h_raw[:, t % 2], ACT.Copy).then_inc(h_hi, 1)

                def step(k, t, more):
                    if more:
                        high(k + (t + 1) // TB, (t + 1) % TB)
                    act.wait_ge(var_done, TB * k + t + 1)
                    act.activation(std[:, t % 2:t % 2 + 1], mv[:, t % 2, 1:2], ACT.Sqrt, bias=eps[:, 0:1]
                                   ).then_inc(std_done, 1)

                act.wait_ge(eps_set, 1)
                high(0, 0)
                for t in range(TB):
                    step(0, t, True)
                with act.Fori(1, LOOPS - 1) as k:
                    for t in range(TB):
                        step(k, t, True)
                for t in range(TB):
                    step(LOOPS - 1, t, t + 1 < TB)

            @block.vector
            def _(dve):
                dve.memset(eps[:, :], EPS).then_inc(eps_set, 1)
                dve.sem_inc(added, 2 * HALVES)
                for n in range(turn_groups):
                    i, half = n // 2, n % 2
                    dve.wait_ge(w_hi, n + 1)
                    at = wd[:, :, 4 * half:4 * half + 4, i * P:(i + 1) * P]
                    dve.tensor_tensor(at[:, 1], psum[:, n % W_BANKS, :].rearrange("p (a t) -> p a t", a=4),
                                      raw(at[:, 0]), ALU.subtract).then_inc(w_lo, 1)

                def low(k, t):
                    dve.wait_ge(h_hi, TB * k + t + 1)
                    dve.tensor_tensor(ht[:, t % 2, 1], h_raw[:, t % 2], raw(ht[:, t % 2, 0]), ALU.subtract
                                      ).then_inc(h_lo, 1)

                def step(k, t, more):
                    if more:
                        low(k + (t + 1) // TB, (t + 1) % TB)
                    par, tile = t % 2, TB * k + t
                    dve.wait_ge(r_in[t], 16 * (k + 1))
                    for half in range(HALVES):
                        cols = slice(half * HW, (half + 1) * HW)
                        dve.wait_ge(done_half, HALVES * tile + half + 1)
                        dve.tensor_tensor(r[:, t, cols], psum[:, BANK0 + HALVES * par + half, :], r[:, t, cols], ALU.add
                                          ).then_inc(added, 1)
                        dve.wait_ge(added, HALVES * tile + half + 1 + 2 * HALVES)
                        dve.bn_stats(stats[:, par, half, :], r[:, t, cols]).then_inc(counted, 1)
                    dve.wait_ge(counted, HALVES * (tile + 1))
                    dve.sem_inc(idle, 1)
                    dve.bn_aggr(mv[:, par, :], stats[:, par].rearrange("p a b -> p (a b)")).then_inc(var_done, 1)
                    dve.wait_ge(std_done, tile + 1)
                    dve.reciprocal(rstd[:, par:par + 1], std[:, par:par + 1]).then_inc(inverted, 1)
                    dve.wait_ge(inverted, tile + 1)
                    dve.tensor_scalar(r[:, t, :], r[:, t, :], mv[:, par, 0:1], rstd[:, par:par + 1], ALU.subtract,
                                      ALU.mult).then_inc(normed, 1)

                low(0, 0)
                with dve.Fori(0, LOOPS - 1) as k:
                    for t in range(TB):
                        step(k, t, True)
                for t in range(TB):
                    step(LOOPS - 1, t, t + 1 < TB)


def post_ln_layer(nc, x, wq, bq, wk, bk, wv, bv, wup, wdown, wg, wex, out):
    dims, dram, const = Names(), Names(), Names()
    dims.B, dims.S, dims.D = x.shape
    dims.H, _, dims.HD = wq.shape
    dims.G = wk.shape[0]
    dims.E = wg.shape[0]
    B, S, D, H, G, HD = dims.B, dims.S, dims.D, dims.H, dims.G, dims.HD

    def scratch(name, *shape):
        return nc.dram_tensor(name, shape, F32, kind="Internal").ap()

    dram.x = x.rearrange("b (i p) n -> (b i) p n", p=P)
    dram.out = out.rearrange("b (i p) n -> (b i) p n", p=P)
    dram.wq, dram.wk, dram.wv = wq, wk, wv
    dram.bq = bq.rearrange("h (d a) -> (h d) a", a=1)
    dram.bk = bk.rearrange("g (d a) -> (g d) a", a=1)
    dram.bv = bv.rearrange("(a g) d -> a (g d)", a=1)
    dram.wup, dram.wdown, dram.wg, dram.wex = wup, wdown, wg, wex
    dram.q = scratch("q_split", B * G, H // G, 2 * HD, S)
    dram.k = scratch("k_split", B * G, 2, HD, S)
    dram.v = scratch("v_split", B * G, S, 2 * HD)
    dram.att = scratch("attention", B, S, G, H // G * HD)
    dram.att_tiles = dram.att.rearrange("b (i p) g n -> (b i) p (g n)", p=P)
    dram.h = scratch("hidden_t", B * S // P, P, D // P, P)
    dram.r = scratch("residual", B * S // P, P, D)

    with ExitStack() as c:
        psum_t = c.enter_context(nc.psum_tensor("banks", [P, 8, 512], F32))
        const.ident = c.enter_context(nc.sbuf_tensor("ident", [P, P], F32))
        const.ident_r = c.enter_context(nc.sbuf_tensor("ident_r", [P, P], F32R))
        const.mask = c.enter_context(nc.sbuf_tensor("mask", [P, P], F32R))
        const.fold = c.enter_context(nc.sbuf_tensor("fold", [P, HD], F32))
        constants(nc, const)
        stage_a(nc, dims, dram, const, psum_t)
        with nc.sbuf_tensor("w_raw_c", [P, D // P, D], F32) as w_raw:
            pass
        const.w_raw = w_raw
        const.yt = [c.enter_context(nc.sbuf_tensor(f"yt{i}", [P, 2, D // P, 2 * P], F32R)) for i in range(2)]
        const.att = c.enter_context(nc.sbuf_tensor("att_sb", [P, 2, D], F32))
        const.wup_in = c.enter_context(nc.semaphore("wup_in"))
        const.wdown_in = c.enter_context(nc.semaphore("wdown_in"))
        stage_b(nc, dims, dram, const, psum_t)
        stage_c(nc, dims, dram, const, psum_t)
        stage_d(nc, dims, dram, const, psum_t)


_INS = ["L0_attn_x", "L0_attn_Wq", "L0_attn_bq", "L0_attn_Wk", "L0_attn_bk", "L0_attn_Wv", "L0_attn_bv",
        "L0_ffn_W_up", "L0_ffn_W_down", "L0_ffn_W_gate", "L0_ffn_W_expert"]


def kernel(**inputs):
    import numpy as _np
    import concourse.bacc as _bacc
    from concourse import mybir as _mybir
    from concourse.bass_utils import run_bass_kernel_spmd as _run

    nc = _bacc.Bacc("TRN2", target_bir_lowering=False, num_devices=1)
    arrays, args = {}, []
    for name in _INS:
        a = _np.ascontiguousarray(inputs[name])
        arrays[f"in_{name}"] = a
        args.append(nc.dram_tensor(f"in_{name}", a.shape, _mybir.dt.from_np(a.dtype), kind="ExternalInput").ap())
    shape = arrays["in_L0_attn_x"].shape
    args.append(nc.dram_tensor("out_dram", shape, _mybir.dt.float32, kind="ExternalOutput").ap())
    post_ln_layer(nc, *args)
    r = _run(nc, [arrays], core_ids=[0])
    return r.results[0]["out_dram"]
```
